# Optimizing a Trainium2 kernel written in Bass

```python
import numpy as np
import jax
import jax.numpy as jnp

def _softmax(x, axis=-1):
    return jax.nn.softmax(x, axis=axis)

def _gelu(x):
    return jax.nn.gelu(x, approximate=True)

def _silu(x):
    return jax.nn.silu(x)

def _sigmoid(x):
    return jax.nn.sigmoid(x)

def _layernorm(x, axis=-1, eps=1e-05):
    m = jnp.mean(x, axis=axis, keepdims=True)
    v = jnp.var(x, axis=axis, keepdims=True)
    return (x - m) / jnp.sqrt(v + eps)

def _scatter_add(tgt, idx, src, axis=0):
    return tgt.at[idx].add(src)

def _segment_sum(src, seg, n):
    return jax.ops.segment_sum(src, seg, n)
kernel_name = 'mk_macaron_d2_jaxref_r8_cb0e10'

def setup_inputs(seed: int=0):
    np.random.seed(seed)
    _w = jnp.asarray

    def _L0_attn_setup():
        import jax, jax.numpy as jnp
        import numpy as np
        B, N, D, H = (4, 256, 128, 16)
        Dh = D // H
        ROPE_THETA = 10000.0

        def _rope(x):
            n, d = (x.shape[-2], x.shape[-1])
            inv_freq = 1.0 / ROPE_THETA ** (jnp.arange(0, d, 2, dtype=jnp.float32) / d)
            freqs = jnp.arange(n, dtype=jnp.float32)[:, None] * inv_freq[None, :]
            freqs = jnp.repeat(freqs, 2, axis=-1)
            cos, sin = (jnp.cos(freqs), jnp.sin(freqs))
            x1 = x[..., ::2]
            x2 = x[..., 1::2]
            rot = jnp.stack([-x2, x1], axis=-1).reshape(x.shape)
            return x * cos + rot * sin
        key = jax.random.key(seed)
        ks = jax.random.split(key, 9)
        s = 0.02
        return {'x': jax.random.normal(ks[0], (B, N, D), dtype=jnp.float32), 'Wq': jax.random.normal(ks[1], (D, D), dtype=jnp.float32) * s, 'bq': jax.random.normal(ks[2], (D,), dtype=jnp.float32) * s, 'Wk': jax.random.normal(ks[3], (D, D), dtype=jnp.float32) * s, 'bk': jax.random.normal(ks[4], (D,), dtype=jnp.float32) * s, 'Wv': jax.random.normal(ks[5], (D, D), dtype=jnp.float32) * s, 'bv': jax.random.normal(ks[6], (D,), dtype=jnp.float32) * s, 'Wo': jax.random.normal(ks[7], (D, D), dtype=jnp.float32) * s, 'bo': jax.random.normal(ks[8], (D,), dtype=jnp.float32) * s}
    _L0_attn_in = _L0_attn_setup()

    def _L0_ffn_setup():
        import jax, jax.numpy as jnp
        import numpy as np
        B, S, H = (8, 128, 128)
        FF = 512
        E = 8
        TOP_K = 2
        LN_EPS = 1e-12

        def _layernorm(x, w, b):
            mu = jnp.mean(x, axis=-1, keepdims=True)
            var = jnp.mean(jnp.square(x - mu), axis=-1, keepdims=True)
            return (x - mu) * jax.lax.rsqrt(var + LN_EPS) * w + b
        key = jax.random.key(seed)
        ks = jax.random.split(key, 8)
        sc_h = 1.0 / np.sqrt(H)
        sc_ff = 1.0 / np.sqrt(FF)
        return {'hidden_states': jax.random.normal(ks[0], (B, S, H), jnp.float32), 'router_w': jax.random.normal(ks[1], (E, H), jnp.float32) * sc_h, 'router_b': jnp.zeros((E,), jnp.float32), 'w1': jax.random.normal(ks[2], (E, FF, H), jnp.float32) * sc_h, 'b1': jax.random.normal(ks[3], (E, FF), jnp.float32) * 0.01, 'w2': jax.random.normal(ks[4], (E, H, FF), jnp.float32) * sc_ff, 'b2': jax.random.normal(ks[5], (E, H), jnp.float32) * 0.01, 'ln_w': jnp.ones((H,), jnp.float32), 'ln_b': jnp.zeros((H,), jnp.float32)}
    _L0_ffn_in = _L0_ffn_setup()

    def _L1_attn_setup():
        import math
        import jax, jax.numpy as jnp
        import numpy as np
        D_MODEL = 128
        N_HEADS = 16
        D_K = D_MODEL // N_HEADS
        D_C = 32
        B, S = (2, 256)
        key = jax.random.key(seed)
        ks = jax.random.split(key, 7)
        sd = lambda fan_in: 1.0 / math.sqrt(fan_in)
        return {'x': jax.random.normal(ks[0], (B, S, D_MODEL), dtype=jnp.float32), 'W_dq': jax.random.uniform(ks[1], (D_MODEL, D_C), minval=-sd(D_MODEL), maxval=sd(D_MODEL), dtype=jnp.float32), 'W_uq': jax.random.uniform(ks[2], (D_C, N_HEADS * D_K), minval=-sd(D_C), maxval=sd(D_C), dtype=jnp.float32), 'W_dkv': jax.random.uniform(ks[3], (D_MODEL, D_C), minval=-sd(D_MODEL), maxval=sd(D_MODEL), dtype=jnp.float32), 'W_uk': jax.random.uniform(ks[4], (D_C, N_HEADS * D_K), minval=-sd(D_C), maxval=sd(D_C), dtype=jnp.float32), 'W_uv': jax.random.uniform(ks[5], (D_C, N_HEADS * D_K), minval=-sd(D_C), maxval=sd(D_C), dtype=jnp.float32), 'W_o': jax.random.uniform(ks[6], (N_HEADS * D_K, D_MODEL), minval=-sd(N_HEADS * D_K), maxval=sd(N_HEADS * D_K), dtype=jnp.float32)}
    _L1_attn_in = _L1_attn_setup()

    def _L1_ffn_setup():
        import jax, jax.numpy as jnp
        import numpy as np
        TOP_K = 2
        CAPACITY_FACTOR = 1.0
        key = jax.random.key(seed)
        ks = jax.random.split(key, 4)
        sl, bs, hs, ffn, E = (256, 8, 128, 512, 8)
        x = jax.random.normal(ks[0], (sl, bs, hs), dtype=jnp.float32)
        w_router = jax.random.normal(ks[1], (hs, E), dtype=jnp.float32) * 0.02
        w1 = jax.random.normal(ks[2], (E, hs, ffn), dtype=jnp.float32) * 0.02
        w2 = jax.random.normal(ks[3], (E, ffn, hs), dtype=jnp.float32) * 0.02
        bias = jnp.zeros((1, 1, hs), dtype=jnp.float32)
        return {'x': x, 'w_router': w_router, 'w1': w1, 'w2': w2, 'bias': bias}
    _L1_ffn_in = _L1_ffn_setup()
    _d = {'L0_attn_x': _L0_attn_in['x'], 'L0_attn_Wq': _L0_attn_in['Wq'], 'L0_attn_bq': _L0_attn_in['bq'], 'L0_attn_Wk': _L0_attn_in['Wk'], 'L0_attn_bk': _L0_attn_in['bk'], 'L0_attn_Wv': _L0_attn_in['Wv'], 'L0_attn_bv': _L0_attn_in['bv'], 'L0_attn_Wo': _L0_attn_in['Wo'], 'L0_attn_bo': _L0_attn_in['bo'], 'L0_ffn_router_w': _L0_ffn_in['router_w'], 'L0_ffn_router_b': _L0_ffn_in['router_b'], 'L0_ffn_w1': _L0_ffn_in['w1'], 'L0_ffn_b1': _L0_ffn_in['b1'], 'L0_ffn_w2': _L0_ffn_in['w2'], 'L0_ffn_b2': _L0_ffn_in['b2'], 'L0_ffn_ln_w': _L0_ffn_in['ln_w'], 'L0_ffn_ln_b': _L0_ffn_in['ln_b'], 'L1_attn_W_dq': _L1_attn_in['W_dq'], 'L1_attn_W_uq': _L1_attn_in['W_uq'], 'L1_attn_W_dkv': _L1_attn_in['W_dkv'], 'L1_attn_W_uk': _L1_attn_in['W_uk'], 'L1_attn_W_uv': _L1_attn_in['W_uv'], 'L1_attn_W_o': _L1_attn_in['W_o'], 'L1_ffn_w_router': _L1_ffn_in['w_router'], 'L1_ffn_w1': _L1_ffn_in['w1'], 'L1_ffn_w2': _L1_ffn_in['w2'], 'L1_ffn_bias': _L1_ffn_in['bias']}
    _x0 = _d['L0_attn_x']
    _d['L0_attn_x'] = jax.random.normal(jax.random.fold_in(jax.random.key(seed), 1), (4, 1024, 128), dtype=_x0.dtype)
    del _x0
    return _d

def reference(L0_attn_x, L0_attn_Wq, L0_attn_bq, L0_attn_Wk, L0_attn_bk, L0_attn_Wv, L0_attn_bv, L0_attn_Wo, L0_attn_bo, L0_ffn_router_w, L0_ffn_router_b, L0_ffn_w1, L0_ffn_b1, L0_ffn_w2, L0_ffn_b2, L0_ffn_ln_w, L0_ffn_ln_b, L1_attn_W_dq, L1_attn_W_uq, L1_attn_W_dkv, L1_attn_W_uk, L1_attn_W_uv, L1_attn_W_o, L1_ffn_w_router, L1_ffn_w1, L1_ffn_w2, L1_ffn_bias):

    def _L0_attn_ref(x, Wq, bq, Wk, bk, Wv, bv, Wo, bo):
        import jax, jax.numpy as jnp
        import numpy as np
        B, N, D, H = (4, 256, 128, 16)
        Dh = D // H
        ROPE_THETA = 10000.0

        def _rope(x):
            n, d = (x.shape[-2], x.shape[-1])
            inv_freq = 1.0 / ROPE_THETA ** (jnp.arange(0, d, 2, dtype=jnp.float32) / d)
            freqs = jnp.arange(n, dtype=jnp.float32)[:, None] * inv_freq[None, :]
            freqs = jnp.repeat(freqs, 2, axis=-1)
            cos, sin = (jnp.cos(freqs), jnp.sin(freqs))
            x1 = x[..., ::2]
            x2 = x[..., 1::2]
            rot = jnp.stack([-x2, x1], axis=-1).reshape(x.shape)
            return x * cos + rot * sin
        b, n, d = x.shape
        split = lambda t: t.reshape(b, n, H, Dh).transpose(0, 2, 1, 3)
        q = split(x @ Wq + bq)
        k = split(x @ Wk + bk)
        v = split(x @ Wv + bv)
        q = _rope(q)
        k = _rope(k)
        scores = jnp.einsum('bhnd,bhmd->bhnm', q, k) / jnp.sqrt(jnp.float32(d))
        weights = jax.nn.softmax(scores, axis=-1)
        inter = jnp.einsum('bhnm,bhmd->bhnd', weights, v)
        inter = inter.transpose(0, 2, 1, 3).reshape(b, n, d)
        return inter @ Wo + bo

    def _L0_ffn_ref(hidden_states, router_w, router_b, w1, b1, w2, b2, ln_w, ln_b):
        import jax, jax.numpy as jnp
        import numpy as np
        B, S, H = (8, 128, 128)
        FF = 512
        E = 8
        TOP_K = 2
        LN_EPS = 1e-12

        def _layernorm(x, w, b):
            mu = jnp.mean(x, axis=-1, keepdims=True)
            var = jnp.mean(jnp.square(x - mu), axis=-1, keepdims=True)
            return (x - mu) * jax.lax.rsqrt(var + LN_EPS) * w + b
        b, s, h = hidden_states.shape
        flat = hidden_states.reshape(-1, h)
        logits = flat @ router_w.T + router_b
        topk_vals, topk_idx = jax.lax.top_k(logits, TOP_K)
        topk_w = jax.nn.softmax(topk_vals, axis=-1)
        out = jnp.zeros_like(flat)
        n_exp = w1.shape[0]
        for e in range(n_exp):
            cw = jnp.sum(jnp.where(topk_idx == e, topk_w, 0.0), axis=-1)
            y = jax.nn.gelu(flat @ w1[e].T + b1[e], approximate=False)
            y = y @ w2[e].T + b2[e]
            out = out + y * cw[:, None]
        out = out.reshape(b, s, h) + hidden_states
        return _layernorm(out, ln_w, ln_b)

    def _L1_attn_ref(x, W_dq, W_uq, W_dkv, W_uk, W_uv, W_o):
        import math
        import jax, jax.numpy as jnp
        import numpy as np
        D_MODEL = 128
        N_HEADS = 16
        D_K = D_MODEL // N_HEADS
        D_C = 32
        B, S = (2, 256)
        Bx, Sx, _ = x.shape
        c_q = x @ W_dq
        Q = (c_q @ W_uq).reshape(Bx, Sx, N_HEADS, D_K)
        c_kv = x @ W_dkv
        K = (c_kv @ W_uk).reshape(Bx, Sx, N_HEADS, D_K)
        V = (c_kv @ W_uv).reshape(Bx, Sx, N_HEADS, D_K)
        scores = jnp.einsum('bqhd,bkhd->bhqk', Q, K) / math.sqrt(D_K)
        causal = jnp.tril(jnp.ones((Sx, Sx), dtype=bool))
        scores = jnp.where(causal, scores, -jnp.inf)
        attn = jax.nn.softmax(scores, axis=-1)
        out = jnp.einsum('bhqk,bkhd->bqhd', attn, V).reshape(Bx, Sx, N_HEADS * D_K)
        return out @ W_o

    def _L1_ffn_ref(x, w_router, w1, w2, bias):
        import jax, jax.numpy as jnp
        import numpy as np
        TOP_K = 2
        CAPACITY_FACTOR = 1.0
        sl, bs, hs = x.shape
        E = w_router.shape[1]
        xf = x.reshape(-1, hs)
        T = xf.shape[0]
        capacity = int(CAPACITY_FACTOR * TOP_K * T / E)
        scores = jax.nn.softmax(xf @ w_router, axis=-1)
        expert_weights, top_experts = jax.lax.top_k(scores, TOP_K)
        flat_e = top_experts.reshape(-1)
        flat_w = expert_weights.reshape(-1)
        N = flat_e.shape[0]
        order = jnp.argsort(flat_e, stable=True)
        bin_ids = flat_e[order]
        tpe = jnp.zeros((E,), jnp.int32).at[flat_e].add(1)
        starts = jnp.cumsum(tpe) - tpe
        offsets = jnp.arange(N) - starts[bin_ids]
        valid = offsets < capacity
        slot = jnp.where(valid, bin_ids * capacity + offsets, E * capacity)
        src = order // TOP_K
        xb = jnp.zeros((E * capacity + 1, hs), x.dtype).at[slot].set(xf[src])
        xb = xb[:-1].reshape(E, capacity, hs)
        h = jax.nn.gelu(jnp.einsum('ech,ehf->ecf', xb, w1))
        y = jnp.einsum('ecf,efh->ech', h, w2).reshape(E * capacity, hs)
        yv = jnp.where(valid[:, None], y[jnp.minimum(slot, E * capacity - 1)], 0.0)
        out = jnp.zeros((T, hs), x.dtype).at[src].add(flat_w[order][:, None] * yv)
        return out.reshape(sl, bs, hs) + bias
    x = L0_attn_x
    x = x + 0.5 * _L0_ffn_ref(_layernorm(x, axis=-1), L0_ffn_router_w, L0_ffn_router_b, L0_ffn_w1, L0_ffn_b1, L0_ffn_w2, L0_ffn_b2, L0_ffn_ln_w, L0_ffn_ln_b)
    x = x + _L0_attn_ref(_layernorm(x, axis=-1), L0_attn_Wq, L0_attn_bq, L0_attn_Wk, L0_attn_bk, L0_attn_Wv, L0_attn_bv, L0_attn_Wo, L0_attn_bo)
    x = x + 0.5 * _L0_ffn_ref(_layernorm(x, axis=-1), L0_ffn_router_w, L0_ffn_router_b, L0_ffn_w1, L0_ffn_b1, L0_ffn_w2, L0_ffn_b2, L0_ffn_ln_w, L0_ffn_ln_b)
    x = x + 0.5 * _L1_ffn_ref(_layernorm(x, axis=-1), L1_ffn_w_router, L1_ffn_w1, L1_ffn_w2, L1_ffn_bias)
    x = x + _L1_attn_ref(_layernorm(x, axis=-1), L1_attn_W_dq, L1_attn_W_uq, L1_attn_W_dkv, L1_attn_W_uk, L1_attn_W_uv, L1_attn_W_o)
    x = x + 0.5 * _L1_ffn_ref(_layernorm(x, axis=-1), L1_ffn_w_router, L1_ffn_w1, L1_ffn_w2, L1_ffn_bias)
    return x

_drawn_inputs = setup_inputs


def setup_inputs(seed=0):
    import zlib

    import numpy as np

    out = dict(_drawn_inputs(seed))
    spreads = {'L0_ffn_router_b': (0.0, 0.1),
     'L0_ffn_ln_w': (1.0, 0.2),
     'L0_ffn_ln_b': (0.0, 0.1),
     'L1_ffn_bias': (0.0, 0.1)}
    factors = {'L0_attn_Wq': 8.0,
     'L0_attn_bq': 8.0,
     'L0_attn_Wk': 8.0,
     'L0_attn_bk': 8.0,
     'L0_attn_Wv': 8.0,
     'L0_attn_bv': 8.0,
     'L0_attn_Wo': 8.0,
     'L0_attn_bo': 3.487,
     'L0_ffn_b1': 8.0,
     'L0_ffn_b2': 8.0,
     'L1_attn_W_dq': 8.0,
     'L1_attn_W_uq': 8.0,
     'L1_attn_W_dkv': 4.873,
     'L1_attn_W_uk': 8.0,
     'L1_attn_W_uv': 5.537,
     'L1_attn_W_o': 4.95,
     'L1_ffn_w_router': 8.0,
     'L1_ffn_w1': 8.0,
     'L1_ffn_w2': 8.0}
    for name, (base, spread) in spreads.items():
        noise = np.random.default_rng([zlib.crc32(name.encode()), seed]).standard_normal(out[name].shape)
        drawn = base * np.exp(spread * noise) if base else spread * noise
        out[name] = jnp.asarray(drawn.astype(out[name].dtype))
    for name, factor in factors.items():
        out[name] = (out[name] * factor).astype(out[name].dtype)
    return out
```

```python
from contextlib import ExitStack

import numpy as np
import concourse.bass as bass
from concourse import mybir
from concourse.alu_op_type import AluOpType as ALU

F32, BF16 = mybir.dt.float32, mybir.dt.bfloat16
ACT, AX = mybir.ActivationFunctionType, mybir.AxisListType
P = 128
B, N, D = 4, 1024, 128
T = B * N
NT = T // P
BLK = 512
NB = T // BLK
TPB = BLK // P
E, FF = 8, 512
NC = FF // P
CAPACITY = 2 * T // E
H, DH = 16, 8
HEADS = B * H
NKT = N // P
PARTS = 3
KQ = PARTS * PARTS * DH
KS = KQ + PARTS
VW = 40
RING = 4
NEG = -1e30
CONST_COLS = 4 * P + E


class Steps:

    def __init__(self, engine, sem):
        self.engine, self.sem, self.n, self.base = engine, sem, 0, 0

    def link(self, instruction):
        instruction.then_inc(self.sem, 1)
        self.n += 1
        self.engine.wait_ge(self.sem, self.base + self.n)

    def loop(self, count, per):
        start = self.n
        with self.engine.Fori(0, count) as i:
            self.base = i * per
            yield i
            assert self.n - start == per, (self.n - start, per)
        self.base, self.n = 0, start + count * per


class Stage:

    def __init__(self, sem, k, stages):
        def new(name):
            return sem(f"{name}_{k}")

        self.k, self.kind = k, stages[k]
        self.loads = len({q for q in stages[:k + 1] if q.startswith("ffn")})
        self.xc_ready = new("xc_ready")
        self.sq_ready = new("sq_ready")
        self.std_in = new("std_in")
        self.std_ready = new("std_ready")
        self.xn_ready = new("xn_ready")
        self.tr_done = new("tr_done")
        self.tr_evac = new("tr_evac")
        if self.kind.startswith("ffn"):
            self.lg_done = new("lg_done")
            self.ex_in = new("ex_in")
            self.ex_ready = new("ex_ready")
            self.sel_ready = new("sel_ready")
            self.cnt_done = new("cnt_done")
            self.gelu_done = new("gelu_done")
            self.down_done = new("down_done")
            self.comb_done = new("comb_done")
        else:
            self.qkv_done = new("qkv_done")
            self.qkv_free = new("qkv_free")
            self.p_copied = new("p_copied")
            self.r_ready = new("r_ready")
            self.parts_ready = new("parts_ready")
            self.v_done = new("v_done")
            self.v_evac = new("v_evac")
            self.c_done = new("c_done")
            self.c_evac = new("c_evac")
            self.st_done = new("st_done")
            self.exp_done = new("exp_done")
            self.pv_done = new("pv_done")
            self.sm_done = new("sm_done")
            self.red_done = new("red_done")
            self.mt_done = new("mt_done")
            self.msplit = new("msplit")
            self.nrm_done = new("nrm_done")
            self.v_ready = new("v_ready")
            self.wo_done = new("wo_done")
            self.wo_free = new("wo_free")
            self.parts_out = [new(f"parts_out{r}") for r in range(2)]
            self.qk_in = [new(f"qk_in{r}") for r in range(RING)]
            self.m_in = [new(f"m_in{r}") for r in range(RING)]
            self.o_out = [new(f"o_out{r}") for r in range(2)]
            self.att_in = [new(f"att_in{r}") for r in range(2)]
            self.scale = float(1 / np.sqrt(np.float32(D if self.kind == "attn0" else DH)))
            self.causal = self.kind == "attn1"
            self.groups = [(hf, kt) for hf in range(2) for kt in range(0, NKT, 2)
                           if not (self.causal and kt >= 4 * (hf + 1))]
            self.G = len(self.groups)
            self.half_end = [sum(h <= hf for h, _ in self.groups) for hf in range(2)]


def bcast(ap, axis, n):
    a = ap.unsqueeze(axis)
    shape = list(a.shape)
    shape[axis] = n
    return a.to_broadcast(shape)


def build(nc, ins, out, stages):
    with ExitStack() as ctx:
        def sb(name, shape, dt=F32):
            return ctx.enter_context(nc.sbuf_tensor(name, shape, dt))

        def sem(name):
            return ctx.enter_context(nc.semaphore(name))

        x = sb("x", [P, NT, D])
        xn = sb("xn", [P, NT, D])
        xnT = sb("xnT", [P, T])
        w1 = sb("w1", [P, E, FF])
        w2 = sb("w2", [P, E, NC, D])
        b1 = sb("b1", [P, E, NC])
        b2p = sb("b2p", [1, PARTS, E * D], BF16)
        rw = [sb(f"rw_{k}", [P, E]) for k in range(2)]
        rb = sb("rb", [P, E])
        ffn_bias = sb("ffn_bias", [P, D])
        lnw, lnb = sb("lnw", [P, D]), sb("lnb", [P, D])
        consts = sb("consts", [P, CONST_COLS])
        ident = consts[:, 0:P]
        first_pref = consts[:, 4 * P:4 * P + E]
        cbf = sb("cbf", [P, 4 * P], BF16)
        ident_bf, tri_bf, maskS, maskT = (cbf[:, k * P:(k + 1) * P] for k in range(4))
        ones_bf = sb("ones_bf", [P, P], BF16)
        mean, var, rstd, t32 = (sb(n, [P, NT]) for n in ("mean", "var", "rstd", "t32"))
        lg, r1, r2, sel1, sel2, cw = (sb(n, [P, NT, E]) for n in ("lg", "r1", "r2", "sel1", "sel2", "cw"))
        top1, top2, pw1, pw2 = (sb(n, [P, NT]) for n in ("top1", "top2", "pw1", "pw2"))
        sel_bf = sb("sel_bf", [P, NT, E], BF16)
        cwb = sb("cwb", [P, TPB, E])
        acc = sb("acc", [P, TPB, D])
        sq = sb("sq", [P, TPB, D])
        work = sb("work", [P, 8192])
        hT = work[:, 0:2 * NC * BLK].rearrange("p (s c t) -> p s c t", s=2, c=NC)
        probs = work[:, 0:4 * 2 * BLK].rearrange("p (s c) -> p s c", s=4)
        qk_f = work[:, 4096:8192].rearrange("p (k t) -> p k t", k=8)
        b2f, b2r = work[0:1, 0:E * D], work[0:1, E * D:2 * E * D]
        trig = sb("trig", [P, 2, N])
        wqkv = sb("wqkv", [P, 5, D])
        bqk = sb("bqk", [P, 4])
        bv, bo, wo = sb("bv", [P, D]), sb("bo", [P, D]), [sb(f"wo_{k}", [P, D]) for k in range(2)]
        wd = sb("wd", [P, 2, 32])
        wu = sb("wu", [32, 3, D])
        parts = sb("parts", [P, 2, PARTS, BLK], BF16)
        vall = sb("vall", [P, HEADS, NKT, DH])
        qs = sb("qs", [P, RING, N], BF16)
        ks = sb("ks", [P, RING, N], BF16)
        vr = sb("vr", [P, RING, NKT, VW])
        rowmax = sb("rowmax", [P, RING, NKT])
        mf = sb("mf", [NKT, 2, P])
        mp = sb("mp", [NKT, RING, PARTS, P], BF16)
        rec = sb("rec", [DH, BLK])
        oT = sb("oT", [DH, 2, BLK])
        att_in = sb("att_in", [P, 2, BLK])
        ckv = xn[0:32, :, :].rearrange("p t d -> p (t d)")
        cq = att_in[0:32, 0, :]

        ps = ctx.enter_context(nc.psum_tensor("ps", [P, 8, BLK], F32))

        qp = nc.dram_tensor("q_parts", [HEADS, PARTS * DH, N], BF16).ap()
        kp = nc.dram_tensor("k_parts", [HEADS, PARTS * DH, N], BF16).ap()
        att = nc.dram_tensor("att_out", [HEADS * DH, N], F32).ap()

        x_in, par_in, w_in, out_done = sem("x_in"), sem("par_in"), sem("w_in"), sem("out_done")
        c_ready = sem("c_ready")
        dve_step = sem("dve_step")
        stage_done = sem("stage_done")

        S = [Stage(sem, k, stages) for k in range(len(stages))]

        block = ctx.enter_context(nc.Block())

        PV0 = 8 * RING

        def sp_attention(sp, s):
            for hf in range(2):
                sp.sem_inc(s.o_out[hf], 16)
            for j in range(NB):
                b, c0 = j // 2, (j % 2) * BLK
                for w, dst in ((0, qp), (1, kp)):
                    sp.wait_ge(s.parts_ready, 2 * j + w + 1)
                    d = dst[b * H:(b + 1) * H, :, c0:c0 + BLK].rearrange("h (a d) t -> a h d t", a=PARTS)
                    for a in range(PARTS):
                        sp.dma_start(d[a], parts[:, w, a, :]).then_inc(s.parts_out[w], 16)
            for w in range(2):
                sp.wait_ge(s.parts_out[w], 16 * NB * PARTS)

            def load(i, r, waits):
                q_src = qp[bass.ds(i * RING + r, 1), :, :].rearrange("o p t -> (o p) t")
                k_src = [kp[bass.ds(i * RING + r, 1), a * DH:(a + 1) * DH, :].rearrange("o p t -> (o p) t")
                         for a in range(PARTS)]
                if waits is not None:
                    sp.wait_ge(s.pv_done, waits)
                for c in range(PARTS):
                    sp.dma_start(qs[c * 24:(c + 1) * 24, r, :], q_src).then_inc(s.qk_in[r], 16)
                for a in range(PARTS):
                    for c in range(PARTS):
                        sp.dma_start(ks[a * 24 + c * 8:a * 24 + c * 8 + 8, r, :], k_src[a]).then_inc(s.qk_in[r], 16)

            def store(i, r, hf):
                dst = att[bass.ds((i * RING + r) * DH, DH), hf * BLK:(hf + 1) * BLK]
                sp.wait_ge(s.nrm_done, (i * RING + r) * 2 + hf + 3)
                sp.dma_start(dst, oT[:, hf, :]).then_inc(s.o_out[hf], 16)

            def max_rows(i, r):
                sp.wait_ge(s.msplit, i * RING + r + 2)
                for a in range(PARTS):
                    sp.dma_start(qs[KQ + a:KQ + a + 1, r, :].rearrange("o (q c) -> o q c", c=P),
                                 mp[:, r, a, :]).then_inc(s.m_in[r], 16)

            def step(i, r, ahead, more):
                store(i, r, 0)
                if ahead:
                    max_rows(i + (r + 1) // RING, (r + 1) % RING)
                store(i, r, 1)
                if more:
                    load(i + 1, r, PV0 + s.G * (i * RING + r + 1))

            for r in range(RING):
                load(0, r, None)
            max_rows(0, 0)
            with sp.Fori(0, HEADS // RING - 1) as i:
                for r in range(RING):
                    step(i, r, True, True)
            for r in range(RING):
                step(HEADS // RING - 1, r, r + 1 < RING, False)
            for hf in range(2):
                sp.wait_ge(s.o_out[hf], 16 * HEADS + 16)
            for j in range(NB):
                b, c0 = j // 2, (j % 2) * BLK
                if j >= 2:
                    sp.wait_ge(s.wo_done, j - 1)
                sp.dma_start(att_in[:, j % 2, :], att[b * P:(b + 1) * P, c0:c0 + BLK]).then_inc(s.att_in[j % 2], 16)

        @block.sync
        def _(sp):
            sp.dma_start(x[:], ins["x"].rearrange("(t p) d -> p t d", p=P)).then_inc(x_in, 16)
            small = [(consts[:], ins["consts"]), (rb[:], ins["rb"].partition_broadcast(P)),
                     (rw[0][:], ins["rw0"]), (rw[1][:], ins["rw1"]), (b1[:], ins["b1"]),
                     (b2f, ins["b2"]), (lnw[:], ins["lnw"].partition_broadcast(P)),
                     (lnb[:], ins["lnb"].partition_broadcast(P)),
                     (ffn_bias[:], ins["ffn_bias"].partition_broadcast(P)),
                     (trig[:], ins["trig"]), (wqkv[:], ins["wqkv"]), (bqk[:], ins["bqk"]),
                     (bv[:], ins["bv"].partition_broadcast(P)), (bo[:], ins["bo"].partition_broadcast(P)),
                     (wo[0][:], ins["wo0"]), (wo[1][:], ins["wo1"]), (wd[:], ins["wd"]), (wu[:], ins["wu"])]
            for dst, src in small:
                sp.dma_start(dst, src).then_inc(par_in, 16)
            assert len(small) == N_SMALL
            layer = None
            for s in S:
                if s.kind.startswith("ffn") and s.kind[3] != layer:
                    if layer is not None:
                        sp.wait_ge(stage_done, s.k)
                    layer = s.kind[3]
                    sp.dma_start(w1[:], ins[f"w1_{layer}"]).then_inc(w_in, 16)
                    sp.dma_start(w2[:], ins[f"w2_{layer}"]).then_inc(w_in, 16)
                if s.kind.startswith("attn"):
                    sp_attention(sp, s)
            sp.wait_ge(stage_done, len(S))
            sp.dma_start(out.rearrange("(t p) d -> p t d", p=P), x[:]).then_inc(out_done, 16)
            sp.wait_ge(out_done, 16)

        def act_norm(act, s):
            for g in range(4):
                act.wait_ge(s.xc_ready, g + 1)
                nc.scalar.activation(xnT[:, g * 1024:(g + 1) * 1024],
                                     xn[:, g * 8:(g + 1) * 8, :].rearrange("p t d -> p (t d)"),
                                     ACT.Square).then_inc(s.sq_ready, 1)
            act.wait_ge(s.std_in, 1)
            nc.scalar.activation(t32[:], var[:], ACT.Sqrt).then_inc(s.std_ready, 1)
            for g in range(NB):
                act.wait_ge(s.tr_done, g + 1)
                nc.scalar.copy(xnT[:, g * BLK:(g + 1) * BLK], ps[:, g % 2, :]).then_inc(s.tr_evac, 1)

        def act_ffn(act, s):
            act_norm(act, s)
            zero = s.kind == "ffn0"
            act.wait_ge(s.ex_in, 1)
            if s.kind == "ffn0":
                nc.scalar.activation(t32[:], top2[:], ACT.Exp).then_inc(s.ex_ready, 1)
            else:
                nc.scalar.activation(r1[:], r1[:], ACT.Exp).then_inc(s.ex_ready, 1)
            act.sem_inc(s.gelu_done, 4)
            if zero:
                act.wait_ge(par_in, 16 * N_SMALL)
            with act.Fori(0, NB) as j:
                for e in range(E):
                    for c in range(NC):
                        act.wait_ge(s.tr_done, NB + j * E * NC + e * NC + c + 1)
                        if c == 0:
                            act.wait_ge(s.down_done, j * E + e + 1)
                        nc.scalar.activation(hT[:, e % 2, c, :], ps[:, c, :],
                                             ACT.Gelu if zero else ACT.Gelu_apprx_tanh,
                                             bias=b1[:, e, c:c + 1] if zero else 0.0).then_inc(s.gelu_done, 1)
            if zero:
                act.wait_ge(s.std_in, 2)
                nc.scalar.activation(t32[:], var[:], ACT.Sqrt).then_inc(s.std_ready, 1)

        def act_attention(act, s):
            act_norm(act, s)
            for j in range(NB):
                if s.kind == "attn1":
                    for w, dst in ((0, cq), (1, ckv[:, j * BLK:(j + 1) * BLK])):
                        act.wait_ge(s.c_done, 2 * j + w + 1)
                        if w == 0 and j >= 1:
                            act.wait_ge(s.qkv_done, j)
                        nc.scalar.copy(dst, ps[0:32, 4 + w, :]).then_inc(s.c_evac, 1)
                for w in range(2):
                    for a in range(2):
                        act.wait_ge(s.r_ready, 4 * j + 2 * w + a + 1)
                        if a == 0 and j >= 1:
                            act.wait_ge(s.parts_out[w], 16 * PARTS * j)
                        nc.scalar.copy(parts[:, w, a, :], qk_f[:, 2 + 2 * w + a, :]).then_inc(s.p_copied, 1)

            def exps(i, r):
                n = i * RING + r
                for g, (hf, kt) in enumerate(s.groups):
                    slot = (s.G * r + g) % 4
                    act.wait_ge(s.st_done, n * s.G + g + 1)
                    act.wait_ge(s.pv_done, PV0 + n * s.G + g - 3)
                    st = ps[:, 2 * (g % 2):2 * (g % 2) + 2, :]
                    pr = probs[:, slot, :].rearrange("p (k q) -> p k q", k=2)
                    lo = [max(0, (kt + m) - 4 * hf) * P if s.causal else 0 for m in range(2)]
                    if lo == [0, 0]:
                        nc.scalar.activation(pr, st, ACT.Exp, scale=s.scale).then_inc(s.exp_done, 1)
                    else:
                        nc.scalar.activation(pr[:, 0, lo[0]:], st[:, 0, lo[0]:], ACT.Exp, scale=s.scale)
                        nc.scalar.activation(pr[:, 1, lo[1]:], st[:, 1, lo[1]:], ACT.Exp,
                                             scale=s.scale).then_inc(s.exp_done, 1)

            act.sem_inc(s.exp_done, 2)
            with act.Fori(0, HEADS // RING) as i:
                for r in range(RING):
                    exps(i, r)

        @block.scalar
        def _(act):
            for s in S:
                (act_ffn if s.kind.startswith("ffn") else act_attention)(act, s)

        def pe_transposes(pe, s, then):
            for g in range(NB):
                pe.wait_ge(s.xn_ready, g + 1)
                if g >= 2:
                    pe.wait_ge(s.tr_evac, g - 1)
                for t in range(TPB):
                    mm = nc.tensor.transpose(ps[:, g % 2, t * P:(t + 1) * P], xn[:, g * TPB + t, :], ident)
                mm.then_inc(s.tr_done, 1)
                if g >= 1:
                    then(g - 1)
            then(NB - 1)

        def pe_ffn(pe, s):
            L = int(s.kind[3])

            def logits(g):
                pe.wait_ge(s.tr_evac, g + 1)
                for t in range(g * TPB, (g + 1) * TPB):
                    mm = nc.tensor.matmul(ps[:, 6, t * E:(t + 1) * E], xnT[:, t * P:(t + 1) * P], rw[L][:],
                                          start=True, stop=True)
                mm.then_inc(s.lg_done, 1)

            pe_transposes(pe, s, logits)
            if L == 1:
                pe.wait_ge(s.sel_ready, 1)
                sel = sel_bf[:].rearrange("p t e -> p (t e)")
                nc.tensor.matmul(ps[:, 6, 0:NT * E], tri_bf, sel, start=True, stop=True)
                nc.tensor.matmul(ps[:, 7, 0:NT * E], ones_bf[:], sel, start=True, stop=True).then_inc(s.cnt_done, 1)
            pe.sem_inc(s.down_done, 2)
            pe.wait_ge(w_in, 16 * 2 * s.loads)

            def up(j, e):
                for c in range(NC):
                    pe.wait_ge(s.gelu_done, (j * E + e) * NC + c + 1)
                    nc.tensor.matmul(ps[:, c, :], w1[:, e, c * P:(c + 1) * P], xnT[:, bass.ds(j * BLK, BLK)],
                                     start=True, stop=True).then_inc(s.tr_done, 1)

            def down(j, e):
                pe.wait_ge(s.gelu_done, (j * E + e) * NC + NC + 4)
                pe.wait_ge(s.comb_done, j * E + e + 1)
                y = ps[:, 4 + e % 2, :]
                if L == 0:
                    for a in range(PARTS):
                        nc.tensor.matmul(y.rearrange("p (t d) -> p t d", d=D), ones_bf[0:1, :],
                                         bcast(b2p[:, a, e * D:(e + 1) * D], 1, TPB),
                                         start=(a == 0), stop=False, skip_group_check=True)
                for t in range(TPB):
                    for c in range(NC):
                        mm = nc.tensor.matmul(y[:, t * D:(t + 1) * D], hT[:, e % 2, c, t * P:(t + 1) * P],
                                              w2[:, e, c, :], start=(L == 1 and c == 0), stop=(c == NC - 1),
                                              skip_group_check=True)
                mm.then_inc(s.down_done, 1)

            with pe.Fori(0, NB) as j:
                up(j, 0)
                for e in range(E):
                    if e + 1 < E:
                        up(j, e + 1)
                    down(j, e)

        def pe_attention(pe, s):
            pe_transposes(pe, s, lambda g: None)
            xb = lambda j: xnT[:, j * BLK:(j + 1) * BLK]
            pe.wait_ge(s.tr_evac, NB)
            if s.kind == "attn0":
                for j in range(NB):
                    if j >= 1:
                        pe.wait_ge(s.qkv_free, 2 * j)
                    for w in range(4):
                        mm = nc.tensor.matmul(ps[:, w, :], wqkv[:, w, :], xb(j), start=True, stop=True)
                    mm.then_inc(s.qkv_done, 1)
            else:
                for j in range(NB):
                    if j >= 1:
                        pe.wait_ge(s.c_evac, 2 * j)
                    for w in range(2):
                        nc.tensor.matmul(ps[0:32, 4 + w, :], wd[:, w, :], xb(j), start=True,
                                         stop=True).then_inc(s.c_done, 1)
                    pe.wait_ge(s.c_evac, 2 * j + 2)
                    if j >= 1:
                        pe.wait_ge(s.qkv_free, 2 * j)
                    nc.tensor.matmul(ps[:, 0, :], wu[:, 0, :], cq, start=True, stop=True)
                    nc.tensor.matmul(ps[:, 2, :], wu[:, 1, :], ckv[:, j * BLK:(j + 1) * BLK], start=True,
                                     stop=True).then_inc(s.qkv_done, 1)
            for j in range(NB):
                if j >= 2:
                    pe.wait_ge(s.v_evac, j - 1)
                for t in range(TPB):
                    c = (j * TPB + t) * P
                    lhs, rhs = (xnT[:, c:c + P], wqkv[:, 4, :]) if s.kind == "attn0" else (ckv[:, c:c + P], wu[:, 2, :])
                    mm = nc.tensor.matmul(ps[:, 6 + j % 2, t * P:(t + 1) * P], lhs, rhs, start=True, stop=True)
                mm.then_inc(s.v_done, 1)
            pe.wait_ge(s.v_evac, NB)
            pe.wait_ge(s.qkv_free, 2 * NB)

            def head_max(i, r, q):
                n = i * RING + r
                if q == 0:
                    pe.wait_ge(s.qk_in[r], 16 * 12 * (i + 1))
                    pe.wait_ge(s.msplit, n + 1)
                pe.wait_ge(s.red_done, n * 8 + q + 1)
                keys = (q + 1) * P if s.causal else N
                for c in range(0, keys, BLK):
                    w = min(BLK, keys - c)
                    diag = s.causal and c + w == keys
                    mm = nc.tensor.matmul(ps[:, 4 + c // BLK, 0:w], qs[0:KQ, r, q * P:(q + 1) * P],
                                          ks[0:KQ, r, c:c + w], start=True, stop=not diag, skip_group_check=True)
                    if diag:
                        mm = nc.tensor.matmul(ps[:, 4 + c // BLK, w - P:w], ident_bf, maskS, start=False, stop=True,
                                              skip_group_check=True)
                mm.then_inc(s.sm_done, 1)

            def turn_max(i, r):
                n = i * RING + r
                pe.wait_ge(s.red_done, n * 8 + 8 + 1)
                nc.tensor.transpose(ps[0:NKT, 4, 0:P], rowmax[:, r, :], ident).then_inc(s.mt_done, 1)

            def scores(i, r, g):
                n, (hf, kt) = i * RING + r, s.groups[g]
                if g == 0:
                    pe.wait_ge(s.m_in[r], 16 * PARTS * (i + 1))
                pe.wait_ge(s.exp_done, n * s.G + g + 1)
                for m in range(2):
                    off = kt + m - 4 * hf
                    diag = s.causal and off >= 0
                    lo = off * P if diag else 0
                    mm = nc.tensor.matmul(ps[:, 2 * (g % 2) + m, lo:BLK], ks[0:KS, r, (kt + m) * P:(kt + m + 1) * P],
                                          qs[0:KS, r, hf * BLK + lo:(hf + 1) * BLK], start=True, stop=not diag,
                                          skip_group_check=True)
                    if diag:
                        mm = nc.tensor.matmul(ps[:, 2 * (g % 2) + m, lo:lo + P], ident_bf, maskT, start=False,
                                              stop=True, skip_group_check=True)
                mm.then_inc(s.st_done, 1)

            def values(i, r, g):
                n, (hf, kt) = i * RING + r, s.groups[g]
                slot = (s.G * r + g) % 4
                pe.wait_ge(s.exp_done, n * s.G + g + 1 + 2)
                if g == 0:
                    pe.wait_ge(s.v_ready, n + 1)
                if kt == 0:
                    pe.wait_ge(s.nrm_done, 2 * n + hf + 1)
                for m in range(2):
                    off = kt + m - 4 * hf
                    lo = max(0, off) * P if s.causal else 0
                    last = kt + m == (4 * hf + 3 if s.causal else NKT - 1)
                    mm = nc.tensor.matmul(ps[0:VW, 6 + hf, lo:BLK], vr[:, r, kt + m, :],
                                          probs[:, slot, m * BLK + lo:(m + 1) * BLK],
                                          start=(kt + m == 0), stop=last, skip_group_check=True)
                mm.then_inc(s.pv_done, 1)

            def step(i, r, ahead):
                nr, ni = (r + 1) % RING, i + (r + 1) // RING
                for g in range(s.G):
                    if ahead and g < 4:
                        head_max(ni, nr, 2 * g)
                    scores(i, r, g)
                    if g:
                        values(i, r, g - 1)
                    if ahead and g < 4:
                        head_max(ni, nr, 2 * g + 1)
                    if ahead and g == 4:
                        turn_max(ni, nr)
                values(i, r, s.G - 1)

            pe.sem_inc(s.pv_done, PV0)
            for q in range(8):
                head_max(0, 0, q)
            turn_max(0, 0)
            with pe.Fori(0, HEADS // RING - 1) as i:
                for r in range(RING):
                    step(i, r, True)
            for r in range(RING):
                step(HEADS // RING - 1, r, r + 1 < RING)
            L = int(s.kind[4])
            for j in range(NB):
                pe.wait_ge(s.att_in[j % 2], 16 * (j // 2 + 1))
                if j >= 2:
                    pe.wait_ge(s.wo_free, j - 1)
                for t in range(TPB):
                    mm = nc.tensor.matmul(ps[:, j % 2, t * P:(t + 1) * P], att_in[:, j % 2, t * P:(t + 1) * P],
                                          wo[L][:], start=True, stop=True)
                mm.then_inc(s.wo_done, 1)

        @block.tensor
        def _(pe):
            pe.wait_ge(c_ready, 1)
            for s in S:
                (pe_ffn if s.kind.startswith("ffn") else pe_attention)(pe, s)

        @block.gpsimd
        def _(pool):
            pool.wait_ge(c_ready, 1)
            for s in S:
                if not s.kind.startswith("attn"):
                    continue
                pool.wait_ge(s.v_evac, NB)

                def feed(i, r):
                    n = i * RING + r
                    pool.wait_ge(s.pv_done, PV0 + s.G * (n - RING + 1))
                    nc.gpsimd.tensor_copy(vr[:, r, :, 0:DH], vall[:, bass.ds(n, 1), :, :].rearrange(
                        "p o k d -> p (o k) d")).then_inc(s.v_ready, 1)

                with pool.Fori(0, HEADS // RING) as i:
                    for r in range(RING):
                        feed(i, r)

        @block.vector
        def _(dve):
            st = Steps(dve, dve_step)
            link = st.link
            v = nc.vector
            dve.wait_ge(par_in, 16 * N_SMALL)
            link(v.memset(ones_bf[:], 1.0))
            link(v.tensor_copy(b2p[:, 0, :], b2f))
            link(v.tensor_tensor(b2r, b2f, b2p[:, 0, :], ALU.subtract))
            link(v.tensor_copy(b2p[:, 1, :], b2r))
            link(v.tensor_tensor(b2p[:, 2, :], b2r, b2p[:, 1, :], ALU.subtract))
            link(v.memset(vr[:], 0.0))
            link(v.memset(vr[:, :, :, 32:VW], 1.0))
            link(v.memset(ks[64:P, :, :], -1.0))
            link(v.tensor_copy(cbf[:], consts[:, 0:4 * P]))
            dve.sem_inc(c_ready, 1)
            dve.wait_ge(x_in, 16)

            def normalise():
                for g in range(4):
                    t = slice(g * 8, (g + 1) * 8)
                    link(v.tensor_reduce(mean[:, t], x[:, t, :], AX.X, ALU.add))
                    link(v.tensor_scalar(mean[:, t], mean[:, t], 1.0 / D, None, ALU.mult))
                    v.tensor_tensor(xn[:, t, :], x[:, t, :], bcast(mean[:, t], 2, D),
                                    ALU.subtract).then_inc(s.xc_ready, 1)
                for g in range(4):
                    dve.wait_ge(s.sq_ready, g + 1)
                    link(v.tensor_reduce(var[:, g * 8:(g + 1) * 8],
                                         xnT[:, g * 1024:(g + 1) * 1024].rearrange("p (t d) -> p t d", d=D),
                                         AX.X, ALU.add))
                v.tensor_scalar(var[:], var[:], 1.0 / D, 1e-5, ALU.mult, ALU.add).then_inc(s.std_in, 1)
                dve.wait_ge(s.std_ready, 1)
                inverse_root()
                for g in range(NB):
                    t = slice(g * TPB, (g + 1) * TPB)
                    v.tensor_tensor(xn[:, t, :], xn[:, t, :], bcast(rstd[:, t], 2, D),
                                    ALU.mult).then_inc(s.xn_ready, 1)

            def inverse_root():
                link(v.reciprocal(rstd[:], t32[:]))
                link(v.tensor_tensor(t32[:], rstd[:], rstd[:], ALU.mult))
                link(v.tensor_tensor(t32[:], t32[:], var[:], ALU.mult))
                link(v.tensor_scalar(t32[:], t32[:], -0.5, 1.5, ALU.mult, ALU.add))
                link(v.tensor_tensor(rstd[:], rstd[:], t32[:], ALU.mult))

            def first_of(dst, value, top):
                link(v.tensor_tensor(r2[:], value, bcast(top[:], 2, E), ALU.is_equal))
                link(v.tensor_tensor(r2[:], r2[:], bcast(first_pref, 1, NT), ALU.mult))
                link(v.tensor_reduce(pw1[:], r2[:], AX.X, ALU.max))
                link(v.tensor_tensor(dst, r2[:], bcast(pw1[:], 2, E), ALU.is_equal))

            def top_two(value):
                link(v.tensor_reduce(top1[:], value, AX.X, ALU.max))
                first_of(sel1[:], value, top1)
                link(v.scalar_tensor_tensor(value, sel1[:], -3e38, value, ALU.mult, ALU.add))
                link(v.tensor_reduce(top2[:], value, AX.X, ALU.max))
                first_of(sel2[:], value, top2)

            def route(s):
                dve.wait_ge(s.lg_done, NB)
                logits = ps[:, 6, 0:NT * E].rearrange("p (t e) -> p t e", e=E)
                if s.kind == "ffn0":
                    link(v.tensor_tensor(lg[:], logits, bcast(rb[:], 1, NT), ALU.add))
                    top_two(lg[:])
                    v.tensor_tensor(top2[:], top2[:], top1[:], ALU.subtract).then_inc(s.ex_in, 1)
                    dve.wait_ge(s.ex_ready, 1)
                    link(v.tensor_scalar(pw1[:], t32[:], 1.0, None, ALU.add))
                    link(v.reciprocal(pw1[:], pw1[:]))
                    link(v.tensor_tensor(pw2[:], pw1[:], t32[:], ALU.mult))
                else:
                    link(v.tensor_copy(lg[:], logits))
                    link(v.tensor_reduce(top1[:], lg[:], AX.X, ALU.max))
                    v.tensor_tensor(r1[:], lg[:], bcast(top1[:], 2, E), ALU.subtract).then_inc(s.ex_in, 1)
                    dve.wait_ge(s.ex_ready, 1)
                    link(v.tensor_reduce(t32[:], r1[:], AX.X, ALU.add))
                    link(v.reciprocal(t32[:], t32[:]))
                    link(v.tensor_tensor(r1[:], r1[:], bcast(t32[:], 2, E), ALU.mult))
                    top_two(r1[:])
                    link(v.tensor_copy(pw1[:], top1[:]))
                    link(v.tensor_copy(pw2[:], top2[:]))
                    v.tensor_tensor(sel_bf[:], sel1[:], sel2[:], ALU.add).then_inc(s.sel_ready, 1)
                    dve.wait_ge(s.cnt_done, 1)
                    tot = ps[:, 7, 0:NT * E].rearrange("p (t e) -> p t e", e=E)
                    a, b = r1, r2
                    link(v.memset(a[:, 0:1, :], 0.0))
                    link(v.tensor_copy(a[:, 1:NT, :], tot[:, 0:NT - 1, :]))
                    k = 1
                    while k < NT:
                        link(v.tensor_copy(b[:, 0:k, :], a[:, 0:k, :]))
                        link(v.tensor_tensor(b[:, k:NT, :], a[:, k:NT, :], a[:, 0:NT - k, :], ALU.add))
                        a, b = b, a
                        k *= 2
                    link(v.tensor_tensor(lg[:], ps[:, 6, 0:NT * E].rearrange("p (t e) -> p t e", e=E), a[:], ALU.add))
                    link(v.tensor_scalar(lg[:], lg[:], float(CAPACITY), None, ALU.is_lt))
                link(v.tensor_tensor(sel1[:], sel1[:], bcast(pw1[:], 2, E), ALU.mult))
                link(v.tensor_tensor(sel2[:], sel2[:], bcast(pw2[:], 2, E), ALU.mult))
                link(v.tensor_tensor(cw[:], sel1[:], sel2[:], ALU.add))
                if s.kind == "ffn1":
                    link(v.tensor_tensor(cw[:], cw[:], lg[:], ALU.mult))

            def ffn(s):
                normalise()
                route(s)
                first = s.kind == "ffn0"
                dve.sem_inc(s.comb_done, 2)
                for j in st.loop(NB, 8 if first else 3):
                    tiles = bass.ds(j * TPB, TPB)
                    link(v.tensor_scalar(cwb[:], cw[:, tiles, :], 1.0, None, ALU.mult))
                    link(v.tensor_scalar(acc[:], xn[:, tiles, :] if first else bcast(ffn_bias[:], 1, TPB), 1.0, None,
                                         ALU.mult))
                    for e in range(E):
                        dve.wait_ge(s.down_done, j * E + e + 3)
                        dve.wait_ge(s.comb_done, j * E + e + 2)
                        for t in range(TPB):
                            ins_ = v.scalar_tensor_tensor(acc[:, t, :], ps[:, 4 + e % 2, t * D:(t + 1) * D],
                                                          cwb[:, t, e:e + 1], acc[:, t, :], ALU.mult, ALU.add)
                        ins_.then_inc(s.comb_done, 1)
                    dve.wait_ge(s.comb_done, j * E + E + 2)
                    if first:
                        link(v.tensor_reduce(cwb[:, :, 0], acc[:], AX.X, ALU.add))
                        link(v.tensor_scalar(cwb[:, :, 0], cwb[:, :, 0], 1.0 / D, None, ALU.mult))
                        link(v.tensor_tensor(acc[:], acc[:], cwb[:, :, 0:1].to_broadcast([P, TPB, D]), ALU.subtract))
                        link(v.tensor_scalar(xn[:, tiles, :], acc[:], 1.0, None, ALU.mult))
                        link(v.tensor_tensor(sq[:], acc[:], acc[:], ALU.mult))
                        link(v.tensor_reduce(var[:, tiles], sq[:], AX.X, ALU.add))
                    else:
                        link(v.scalar_tensor_tensor(x[:, tiles, :], acc[:], 0.5, x[:, tiles, :], ALU.mult, ALU.add))
                if first:
                    link(v.tensor_scalar(var[:], var[:], 1.0 / D, 1e-12, ALU.mult, ALU.add))
                    v.tensor_copy(var[:], var[:]).then_inc(s.std_in, 1)
                    dve.wait_ge(s.std_ready, 2)
                    inverse_root()
                    link(v.tensor_tensor(xn[:], xn[:], bcast(rstd[:], 2, D), ALU.mult))
                    link(v.tensor_tensor(xn[:], xn[:], bcast(lnw[:], 1, NT), ALU.mult))
                    link(v.tensor_tensor(xn[:], xn[:], bcast(lnb[:], 1, NT), ALU.add))
                    link(v.scalar_tensor_tensor(x[:], xn[:], 0.5, x[:], ALU.mult, ALU.add))

            def split(s, j, w):
                f, rest = qk_f[:, 2 + 2 * w, :], qk_f[:, 3 + 2 * w, :]
                m = 2 * j + w
                dve.wait_ge(s.p_copied, 2 * m + 1)
                v.tensor_tensor(rest, f, parts[:, w, 0, :], ALU.subtract).then_inc(s.r_ready, 1)
                dve.wait_ge(s.r_ready, 2 * m + 2)
                dve.wait_ge(s.p_copied, 2 * m + 2)
                v.tensor_tensor(parts[:, w, 2, :], rest, parts[:, w, 1, :], ALU.subtract).then_inc(s.parts_ready, 1)

            def attention(s):
                normalise()
                rope = s.kind == "attn0"
                for j in range(NB):
                    pos = slice((j % 2) * BLK, (j % 2) * BLK + BLK)
                    for w in range(2):
                        dve.wait_ge(s.qkv_done, j + 1)
                        if j >= 1:
                            dve.wait_ge(s.parts_ready, 2 * (j - 1) + w + 1)
                        if rope:
                            link(v.scalar_tensor_tensor(qk_f[:, 0, :], ps[:, 2 * w, :], bqk[:, 2 * w:2 * w + 1],
                                                        trig[:, 0, pos], ALU.add, ALU.mult))
                            ins_ = v.scalar_tensor_tensor(qk_f[:, 1, :], ps[:, 2 * w + 1, :],
                                                          bqk[:, 2 * w + 1:2 * w + 2], trig[:, 1, pos],
                                                          ALU.add, ALU.mult)
                            ins_.then_inc(s.qkv_free, 1)
                            dve.wait_ge(s.qkv_free, 2 * j + w + 1)
                            v.tensor_tensor(qk_f[:, 2 + 2 * w, :], qk_f[:, 0, :], qk_f[:, 1, :],
                                            ALU.add).then_inc(s.r_ready, 1)
                        else:
                            link(v.tensor_copy(qk_f[:, 2 + 2 * w, :], ps[:, 2 * w, :]))
                            dve.sem_inc(s.qkv_free, 1)
                            dve.sem_inc(s.r_ready, 1)
                        dve.wait_ge(s.r_ready, 4 * j + 2 * w + 1)
                        split(s, j, w)
                for j in range(NB):
                    dve.wait_ge(s.v_done, j + 1)
                    b, k0 = j // 2, (j % 2) * TPB
                    dst = vall[:, b * H:(b + 1) * H, k0:k0 + TPB, :].rearrange("p h k d -> p k h d")
                    src = ps[:, 6 + j % 2, :].rearrange("p (k h d) -> p k h d", k=TPB, h=H)
                    for k in range(TPB):
                        if rope:
                            ins_ = v.tensor_tensor(dst[:, k], src[:, k], bv[:].rearrange("p (h d) -> p h d", h=H), ALU.add)
                        else:
                            ins_ = v.tensor_copy(dst[:, k], src[:, k])
                    ins_.then_inc(s.v_evac, 1)

                def reduce(i, r, q):
                    n = i * RING + r
                    dve.wait_ge(s.sm_done, n * 8 + q + 1)
                    keys = (q + 1) * P if s.causal else N
                    v.tensor_reduce(rowmax[:, r, q:q + 1],
                                    ps[:, 4:6, :].rearrange("p a c -> p (a c)")[:, 0:keys],
                                    AX.X, ALU.max).then_inc(s.red_done, 1)

                def split_max(i, r):
                    n = i * RING + r
                    dve.wait_ge(s.mt_done, n + 1)
                    link(v.tensor_copy(mf[:, 0, :], ps[0:NKT, 4, 0:P]))
                    link(v.tensor_copy(mp[:, r, 0, :], mf[:, 0, :]))
                    link(v.tensor_tensor(mf[:, 1, :], mf[:, 0, :], mp[:, r, 0, :], ALU.subtract))
                    link(v.tensor_copy(mp[:, r, 1, :], mf[:, 1, :]))
                    v.tensor_tensor(mp[:, r, 2, :], mf[:, 1, :], mp[:, r, 1, :], ALU.subtract).then_inc(s.msplit, 1)

                def divide(i, r, hf):
                    n = i * RING + r
                    dve.wait_ge(s.pv_done, PV0 + n * s.G + s.half_end[hf])
                    dve.wait_ge(s.o_out[hf], 16 * n + 16)
                    dve.wait_ge(s.nrm_done, 2 * n + hf + 2)
                    link(v.reciprocal(rec[:], ps[32:VW, 6 + hf, :]))
                    v.tensor_tensor(oT[:, hf, :], ps[0:DH, 6 + hf, :], rec[:], ALU.mult).then_inc(s.nrm_done, 1)

                def step(i, r, ahead):
                    nr, ni = (r + 1) % RING, i + (r + 1) // RING
                    if ahead:
                        for q in range(8):
                            reduce(ni, nr, q)
                    divide(i, r, 0)
                    if ahead:
                        split_max(ni, nr)
                    divide(i, r, 1)

                dve.sem_inc(s.nrm_done, 2)
                dve.sem_inc(s.msplit, 1)
                dve.sem_inc(s.red_done, 1)
                for q in range(8):
                    reduce(0, 0, q)
                split_max(0, 0)
                for i in st.loop(HEADS // RING - 1, 6 * RING):
                    for r in range(RING):
                        step(i, r, True)
                for r in range(RING):
                    step(HEADS // RING - 1, r, r + 1 < RING)
                for j in range(NB):
                    dve.wait_ge(s.wo_done, j + 1)
                    t = slice(j * TPB, (j + 1) * TPB)
                    src = ps[:, j % 2, :].rearrange("p (t d) -> p t d", d=D)
                    if rope:
                        link(v.tensor_tensor(x[:, t, :], x[:, t, :], bcast(bo[:], 1, TPB), ALU.add))
                    v.tensor_tensor(x[:, t, :], src, x[:, t, :], ALU.add).then_inc(s.wo_free, 1)
                dve.wait_ge(s.wo_free, NB)

            for s in S:
                (ffn if s.kind.startswith("ffn") else attention)(s)
                dve.sem_inc(stage_done, 1)


N_SMALL = 18
STAGES = ("ffn0", "attn0", "ffn0", "ffn1", "attn1", "ffn1")


def constants():
    p, c = np.arange(P)[:, None], np.arange(P)[None, :]
    consts = np.zeros((P, CONST_COLS), np.float32)
    consts[:, 0:P] = p == c
    consts[:, P:2 * P] = p < c
    consts[:, 2 * P:3 * P] = np.where(c > p, NEG, 0)
    consts[:, 3 * P:4 * P] = np.where(p > c, NEG, 0)
    consts[:, 4 * P:] = E - np.arange(E)[None, :]
    inv = (1.0 / np.float32(10000.0) ** (np.arange(0, DH, 2, dtype=np.float32) / np.float32(DH))).astype(np.float32)
    ang = np.repeat(np.arange(N, dtype=np.float32)[:, None] * inv[None, :], 2, axis=-1)
    sign = np.where(np.arange(DH) % 2 == 0, -1.0, 1.0).astype(np.float32)
    cos, sin = np.cos(ang).astype(np.float32), (np.sin(ang) * sign).astype(np.float32)
    trig = np.stack([np.tile(cos.T, (H, 1)), np.tile(sin.T, (H, 1))], axis=1)
    return consts, np.ascontiguousarray(trig)


def kernel(**inputs):
    import concourse.bacc as bacc
    from concourse.bass_utils import run_bass_kernel_spmd as run

    a = {k: np.asarray(v) for k, v in inputs.items()}
    swap = np.arange(D) ^ 1
    consts, trig = constants()
    wq, wk, wv = (a[f"L0_attn_W{k}"] for k in "qkv")
    bq, bk = a["L0_attn_bq"], a["L0_attn_bk"]
    arrays = {
        "x": a["L0_attn_x"].reshape(T, D),
        "consts": consts,
        "trig": trig,
        "rb": a["L0_ffn_router_b"],
        "rw0": a["L0_ffn_router_w"].T,
        "rw1": a["L1_ffn_w_router"],
        "b1": a["L0_ffn_b1"].reshape(E, NC, P).transpose(2, 0, 1),
        "b2": a["L0_ffn_b2"].reshape(1, E * D),
        "lnw": a["L0_ffn_ln_w"],
        "lnb": a["L0_ffn_ln_b"],
        "ffn_bias": a["L1_ffn_bias"].reshape(D),
        "w1_0": a["L0_ffn_w1"].transpose(2, 0, 1),
        "w2_0": a["L0_ffn_w2"].reshape(E, D, NC, P).transpose(3, 0, 2, 1),
        "w1_1": a["L1_ffn_w1"].transpose(1, 0, 2),
        "w2_1": a["L1_ffn_w2"].reshape(E, NC, P, D).transpose(2, 0, 1, 3),
        "wqkv": np.stack([wq, wq[:, swap], wk, wk[:, swap], wv], axis=1),
        "bqk": np.stack([bq, bq[swap], bk, bk[swap]], axis=1),
        "bv": a["L0_attn_bv"],
        "bo": a["L0_attn_bo"],
        "wo0": a["L0_attn_Wo"],
        "wo1": a["L1_attn_W_o"],
        "wd": np.stack([a["L1_attn_W_dq"], a["L1_attn_W_dkv"]], axis=1),
        "wu": np.stack([a["L1_attn_W_uq"], a["L1_attn_W_uk"], a["L1_attn_W_uv"]], axis=1),
    }
    nc = bacc.Bacc("TRN2", target_bir_lowering=False, num_devices=1)
    maps, ins = {}, {}
    for name, v in arrays.items():
        v = np.ascontiguousarray(v)
        maps[f"in_{name}"] = v
        ins[name] = nc.dram_tensor(f"in_{name}", v.shape, mybir.dt.from_np(v.dtype), kind="ExternalInput").ap()
    out = nc.dram_tensor("out", (T, D), F32, kind="ExternalOutput").ap()
    build(nc, ins, out, STAGES)
    r = run(nc, [maps], core_ids=[0])
    return r.results[0]["out"].reshape(B, N, D)
```

```python
from contextlib import ExitStack

import numpy as np
import concourse.bass as bass
from concourse import mybir
from concourse.alu_op_type import AluOpType as ALU

F32, BF16, F16 = mybir.dt.float32, mybir.dt.bfloat16, mybir.dt.float16
ACT, AX = mybir.ActivationFunctionType, mybir.AxisListType
P = 128
B, N, D = 4, 1024, 128
T = B * N
NT = T // P
BLK = 512
NB = T // BLK
TPB = BLK // P
E, FF = 8, 512
NC = FF // P
CAPACITY = 2 * T // E
H, DH = 16, 8
HEADS = B * H
NKT = N // P
PARTS = 3
KQ = PARTS * PARTS * DH
KS = KQ + PARTS
VW = PARTS * DH + 1
SHIFT = 10.0
LAG = 2
W_RING = 4
RING = 4
NEG = -1e30
CONST_COLS = 4 * P + E
LOADS = 2 + PARTS
POOL_F, POOL_C = (1, 3, 5, 7), (1, 3, 5)


class Steps:

    def __init__(self, engine, sem):
        self.engine, self.sem, self.n, self.base = engine, sem, 0, 0

    def link(self, instruction):
        instruction.then_inc(self.sem, 1)
        self.n += 1
        self.engine.wait_ge(self.sem, self.base + self.n)

    def loop(self, count, per):
        start = self.n
        with self.engine.Fori(0, count) as i:
            self.base = i * per
            yield i
            assert self.n - start == per, (self.n - start, per)
        self.base, self.n = 0, start + count * per


def rounds(engine_loop, step):
    last = HEADS // RING - 1
    step(0, 0, 2)
    for i in engine_loop(last):
        for r in range(1, RING):
            step(i, r, 2)
        step(i + 1, 0, 2)
    for r in range(1, RING):
        step(last, r, min(2, RING - 1 - r))


class Stage:

    def __init__(self, sem, k, stages):
        def new(name):
            return sem(f"{name}_{k}")

        self.k, self.kind = k, stages[k]
        self.loads = len({q for q in stages[:k + 1] if q.startswith("ffn")})
        self.xc_ready = new("xc_ready")
        self.sq_ready = new("sq_ready")
        self.std_in = new("std_in")
        self.std_ready = new("std_ready")
        self.xn_ready = new("xn_ready")
        self.tr_done = new("tr_done")
        self.tr_evac = new("tr_evac")
        if self.kind.startswith("ffn"):
            self.lg_done = new("lg_done")
            self.ex_in = new("ex_in")
            self.ex_ready = new("ex_ready")
            self.sel_ready = new("sel_ready")
            self.cnt_done = new("cnt_done")
            self.gelu_done = new("gelu_done")
            self.down_done = new("down_done")
            self.comb_done = new("comb_done")
        else:
            self.qkv_done = new("qkv_done")
            self.qkv_free = new("qkv_free")
            self.p_copied = new("p_copied")
            self.r_ready = new("r_ready")
            self.parts_ready = new("parts_ready")
            self.v_done = new("v_done")
            self.v_evac = new("v_evac")
            self.c_done = new("c_done")
            self.c_evac = new("c_evac")
            self.st_done = new("st_done")
            self.exp_done = new("exp_done")
            self.pv_done = new("pv_done")
            self.sm_done = new("sm_done")
            self.red_done = new("red_done")
            self.row_done = new("row_done")
            self.mt_done = new("mt_done")
            self.msplit = new("msplit")
            self.nrm_done = new("nrm_done")
            self.sub_dve = new("sub_dve")
            self.sub_pool = new("sub_pool")
            self.at_done = new("at_done")
            self.at_evac = new("at_evac")
            self.wo_done = new("wo_done")
            self.wo_free = new("wo_free")
            self.parts_out = [new(f"parts_out{r}") for r in range(2)]
            self.qk_in = [new(f"qk_in{r}") for r in range(RING)]
            self.m_in = [new(f"m_in{r}") for r in range(RING)]
            self.scale = float(1 / np.sqrt(np.float32(D if self.kind == "attn0" else DH)))
            self.causal = self.kind == "attn1"
            self.groups = [(hf, kt) for hf in range(2) for kt in range(0, NKT, 2)
                           if not (self.causal and kt >= 4 * (hf + 1))]
            self.G = len(self.groups)
            self.on_pool = POOL_C if self.causal else POOL_F
            self.on_dve = tuple(g for g in range(self.G) if g not in self.on_pool)
            tiles = ((0, 1, 2), (3,), (4,), (5,), (6,), (7,)) if self.causal else tuple((q,) for q in range(NKT))
            self.pieces, m = [], 0
            for qs in tiles:
                own = []
                for q in qs:
                    keys = (q + 1) * P if self.causal else N
                    for c in range(0, keys, BLK):
                        own.append((m, q, c, min(BLK, keys - c)))
                        m += 1
                self.pieces.append(own)
            self.all_pieces = [p for own in self.pieces for p in own]
            self.M = m


def bcast(ap, axis, n):
    a = ap.unsqueeze(axis)
    shape = list(a.shape)
    shape[axis] = n
    return a.to_broadcast(shape)


def build(nc, ins, out, stages):
    with ExitStack() as ctx:
        def sb(name, shape, dt=F32):
            return ctx.enter_context(nc.sbuf_tensor(name, shape, dt))

        def sem(name):
            return ctx.enter_context(nc.semaphore(name))

        x = sb("x", [P, NT, D])
        xn = sb("xn", [P, NT, D])
        xnT = sb("xnT", [P, T])
        w1 = sb("w1", [P, E, FF])
        w2 = sb("w2", [P, E, NC, D])
        b1 = sb("b1", [P, E, NC])
        b2p = sb("b2p", [1, PARTS, E * D], BF16)
        rw = [sb(f"rw_{k}", [P, E]) for k in range(2)]
        rb = sb("rb", [P, E])
        ffn_bias = sb("ffn_bias", [P, D])
        lnw, lnb = sb("lnw", [P, D]), sb("lnb", [P, D])
        consts = sb("consts", [P, CONST_COLS])
        ident = consts[:, 0:P]
        first_pref = consts[:, 4 * P:4 * P + E]
        cbf = sb("cbf", [P, 4 * P], BF16)
        ident_bf, tri_bf, maskS, maskT = (cbf[:, k * P:(k + 1) * P] for k in range(4))
        ones_bf = sb("ones_bf", [P, P], BF16)
        mean, var, rstd, t32 = (sb(n, [P, NT]) for n in ("mean", "var", "rstd", "t32"))
        lg, r1, r2, sel1, sel2, cw = (sb(n, [P, NT, E]) for n in ("lg", "r1", "r2", "sel1", "sel2", "cw"))
        top1, top2, pw1, pw2 = (sb(n, [P, NT]) for n in ("top1", "top2", "pw1", "pw2"))
        sel_bf = sb("sel_bf", [P, NT, E], BF16)
        cwb = sb("cwb", [P, TPB, E])
        acc = sb("acc", [P, TPB, D])
        sq = sb("sq", [P, TPB, D])
        work = sb("work", [P, 8192])
        hT = work[:, 0:2 * NC * BLK].rearrange("p (s c t) -> p s c t", s=2, c=NC)
        ws = work[:, 0:4096].rearrange("p (s c) -> p s c", s=W_RING)
        wp = work[:, 4096:8192].bitcast(F16).rearrange("p (a s c) -> p a s c", a=2, s=W_RING)
        qk_f = work[:, 4096:8192].rearrange("p (k t) -> p k t", k=8)
        b2f, b2r = work[0:1, 0:E * D], work[0:1, E * D:2 * E * D]
        trig = sb("trig", [P, 2, N])
        wqkv = sb("wqkv", [P, 5, D])
        bqk = sb("bqk", [P, 4])
        bv, bo, wo = sb("bv", [P, D]), sb("bo", [P, D]), [sb(f"wo_{k}", [P, D]) for k in range(2)]
        wd = sb("wd", [P, 2, 32])
        wu = sb("wu", [32, 3, D])
        parts = sb("parts", [P, 2, PARTS, BLK], BF16)
        vall = sb("vall", [P, HEADS, NKT, VW], BF16)
        qs = sb("qs", [P, RING, N], BF16)
        ks = sb("ks", [P, RING, N], BF16)
        vr = sb("vr", [P, RING, NKT, VW], BF16)
        rowmax = sb("rowmax", [P, RING, 2, NKT])
        mf = sb("mf", [NKT, 2, P])
        mp = sb("mp", [NKT, RING, PARTS, P], BF16)
        osum = sb("osum", [P, NKT, DH])
        rec = sb("rec", [P, NKT])
        cq = sb("cq", [32, BLK])
        ckv = xn[0:32, :, :].rearrange("p t d -> p (t d)")

        ps = ctx.enter_context(nc.psum_tensor("ps", [P, 8, BLK], F32))

        qp = nc.dram_tensor("q_parts", [HEADS, PARTS * DH, N], BF16).ap()
        kp = nc.dram_tensor("k_parts", [HEADS, PARTS * DH, N], BF16).ap()

        x_in, par_in, w_in, out_done = sem("x_in"), sem("par_in"), sem("w_in"), sem("out_done")
        c_ready = sem("c_ready")
        dve_step = sem("dve_step")
        stage_done = sem("stage_done")

        S = [Stage(sem, k, stages) for k in range(len(stages))]

        block = ctx.enter_context(nc.Block())

        PV0 = 8 * RING

        def spans(s, hf, kt):
            lo = [max(0, kt + m - 4 * hf) * P if s.causal else 0 for m in range(2)]
            return [(0, 0, 2)] if lo == [0, 0] else [(0, lo[0], 1), (1, lo[1], 1)]

        def span_of(tile, m, lo, w):
            return tile.rearrange("p (k q) -> p k q", k=2)[:, m:m + w, lo:BLK]

        def subtract(engine, s, r, g, done):
            slot = (s.G * r + g) % W_RING
            for m, lo, w in spans(s, *s.groups[g]):
                last = engine.tensor_tensor(span_of(wp[:, 1, slot, :], m, lo, w), span_of(ws[:, slot, :], m, lo, w),
                                            span_of(wp[:, 0, slot, :], m, lo, w), ALU.subtract)
            last.then_inc(done, 1)

        def sp_attention(sp, s):
            for j in range(NB):
                b, c0 = j // 2, (j % 2) * BLK
                for w, dst in ((0, qp), (1, kp)):
                    sp.wait_ge(s.parts_ready, 2 * j + w + 1)
                    d = dst[b * H:(b + 1) * H, :, c0:c0 + BLK].rearrange("h (a d) t -> a h d t", a=PARTS)
                    for a in range(PARTS):
                        sp.dma_start(d[a], parts[:, w, a, :]).then_inc(s.parts_out[w], 16)
            for w in range(2):
                sp.wait_ge(s.parts_out[w], 16 * NB * PARTS)

            def load(i, r, waits):
                n = i * RING + r
                q_src = qp[bass.ds(n, 1), :, :].rearrange("o p t -> (o p) t")
                k_src = [kp[bass.ds(n, 1), a * DH:(a + 1) * DH, :].rearrange("o p t -> (o p) t")
                         for a in range(PARTS)]
                v_src = vall[:, bass.ds(n, 1), :, :].rearrange("p o k d -> p (o k) d")
                if waits is not None:
                    sp.wait_ge(s.pv_done, waits)
                sp.dma_start(qs[0:KQ, r, :], bcast(q_src, 0, PARTS)).then_inc(s.qk_in[r], 16)
                for a in range(PARTS):
                    sp.dma_start(ks[a * 24:(a + 1) * 24, r, :], bcast(k_src[a], 0, PARTS)).then_inc(s.qk_in[r], 16)
                sp.dma_start(vr[:, r, :, :], v_src).then_inc(s.qk_in[r], 16)

            def max_rows(i, r):
                sp.wait_ge(s.msplit, i * RING + r + 2)
                for a in range(PARTS):
                    sp.dma_start(qs[KQ + a:KQ + a + 1, r, :].rearrange("o (q c) -> o q c", c=P),
                                 mp[:, r, a, :]).then_inc(s.m_in[r], 16)

            def step(i, r, ahead, more):
                if ahead:
                    max_rows(i + (r + 1) // RING, (r + 1) % RING)
                if more:
                    load(i + 1, r, PV0 + s.G * (i * RING + r + 1))

            sp.wait_ge(s.v_evac, 2 * NB)
            for r in range(RING):
                load(0, r, None)
            max_rows(0, 0)
            with sp.Fori(0, HEADS // RING - 1) as i:
                for r in range(RING):
                    step(i, r, True, True)
            for r in range(RING):
                step(HEADS // RING - 1, r, r + 1 < RING, False)
        @block.sync
        def _(sp):
            sp.dma_start(x[:], ins["x"].rearrange("(t p) d -> p t d", p=P)).then_inc(x_in, 16)
            small = [(consts[:], ins["consts"]), (rb[:], ins["rb"].partition_broadcast(P)),
                     (rw[0][:], ins["rw0"]), (rw[1][:], ins["rw1"]), (b1[:], ins["b1"]),
                     (b2f, ins["b2"]), (lnw[:], ins["lnw"].partition_broadcast(P)),
                     (lnb[:], ins["lnb"].partition_broadcast(P)),
                     (ffn_bias[:], ins["ffn_bias"].partition_broadcast(P)),
                     (trig[:], ins["trig"]), (wqkv[:], ins["wqkv"]), (bqk[:], ins["bqk"]),
                     (bv[:], ins["bv"].partition_broadcast(P)), (bo[:], ins["bo"].partition_broadcast(P)),
                     (wo[0][:], ins["wo0"]), (wo[1][:], ins["wo1"]), (wd[:], ins["wd"]), (wu[:], ins["wu"])]
            for dst, src in small:
                sp.dma_start(dst, src).then_inc(par_in, 16)
            assert len(small) == N_SMALL
            layer = None
            for s in S:
                if s.kind.startswith("ffn") and s.kind[3] != layer:
                    if layer is not None:
                        sp.wait_ge(stage_done, s.k)
                    layer = s.kind[3]
                    sp.dma_start(w1[:], ins[f"w1_{layer}"]).then_inc(w_in, 16)
                    sp.dma_start(w2[:], ins[f"w2_{layer}"]).then_inc(w_in, 16)
                if s.kind.startswith("attn"):
                    sp_attention(sp, s)
            sp.wait_ge(stage_done, len(S))
            sp.dma_start(out.rearrange("(t p) d -> p t d", p=P), x[:]).then_inc(out_done, 16)
            sp.wait_ge(out_done, 16)

        def act_norm(act, s):
            for g in range(4):
                act.wait_ge(s.xc_ready, g + 1)
                nc.scalar.activation(xnT[:, g * 1024:(g + 1) * 1024],
                                     xn[:, g * 8:(g + 1) * 8, :].rearrange("p t d -> p (t d)"),
                                     ACT.Square).then_inc(s.sq_ready, 1)
            act.wait_ge(s.std_in, 1)
            nc.scalar.activation(t32[:], var[:], ACT.Sqrt).then_inc(s.std_ready, 1)
            for g in range(NB):
                act.wait_ge(s.tr_done, g + 1)
                nc.scalar.copy(xnT[:, g * BLK:(g + 1) * BLK], ps[:, g % 2, :]).then_inc(s.tr_evac, 1)

        def act_ffn(act, s):
            act_norm(act, s)
            zero = s.kind == "ffn0"
            act.wait_ge(s.ex_in, 1)
            if s.kind == "ffn0":
                nc.scalar.activation(t32[:], top2[:], ACT.Exp).then_inc(s.ex_ready, 1)
            else:
                nc.scalar.activation(r1[:], r1[:], ACT.Exp).then_inc(s.ex_ready, 1)
            act.sem_inc(s.gelu_done, 4)
            if zero:
                act.wait_ge(par_in, 16 * N_SMALL)
            with act.Fori(0, NB) as j:
                for e in range(E):
                    for c in range(NC):
                        act.wait_ge(s.tr_done, NB + j * E * NC + e * NC + c + 1)
                        if c == 0:
                            act.wait_ge(s.down_done, j * E + e + 1)
                        nc.scalar.activation(hT[:, e % 2, c, :], ps[:, c, :],
                                             ACT.Gelu if zero else ACT.Gelu_apprx_tanh,
                                             bias=b1[:, e, c:c + 1] if zero else 0.0).then_inc(s.gelu_done, 1)
            if zero:
                act.wait_ge(s.std_in, 2)
                nc.scalar.activation(t32[:], var[:], ACT.Sqrt).then_inc(s.std_ready, 1)

        def act_attention(act, s):
            act_norm(act, s)
            for j in range(NB):
                if s.kind == "attn1":
                    for w, dst in ((0, cq[:]), (1, ckv[:, j * BLK:(j + 1) * BLK])):
                        act.wait_ge(s.c_done, 2 * j + w + 1)
                        if w == 0 and j >= 1:
                            act.wait_ge(s.qkv_done, j)
                        nc.scalar.copy(dst, ps[0:32, 4 + w, :]).then_inc(s.c_evac, 1)
                for w in range(2):
                    for a in range(2):
                        act.wait_ge(s.r_ready, 4 * j + 2 * w + a + 1)
                        if a == 0 and j >= 1:
                            act.wait_ge(s.parts_out[w], 16 * PARTS * j)
                        nc.scalar.copy(parts[:, w, a, :], qk_f[:, 2 + 2 * w + a, :]).then_inc(s.p_copied, 1)

            def exps(i, r):
                n = i * RING + r
                for g, (hf, kt) in enumerate(s.groups):
                    slot = (s.G * r + g) % W_RING
                    act.wait_ge(s.st_done, n * s.G + g + 1)
                    act.wait_ge(s.pv_done, PV0 + n * s.G + g - 3)
                    for m, lo, w in spans(s, hf, kt):
                        st = ps[:, 2 * (g % 2) + m:2 * (g % 2) + m + w, lo:BLK]
                        nc.scalar.activation(span_of(ws[:, slot, :], m, lo, w), st, ACT.Exp,
                                             scale=s.scale)
                        last = nc.scalar.activation(span_of(wp[:, 0, slot, :], m, lo, w), st, ACT.Exp,
                                                    scale=s.scale)
                    last.then_inc(s.exp_done, 1)

            act.sem_inc(s.exp_done, 2)
            with act.Fori(0, HEADS // RING) as i:
                for r in range(RING):
                    exps(i, r)
            for j in range(NB):
                act.wait_ge(s.at_done, j + 1)
                nc.scalar.copy(xnT[:, j * BLK:(j + 1) * BLK], ps[:, j % 2, :]).then_inc(s.at_evac, 1)

        @block.scalar
        def _(act):
            for s in S:
                (act_ffn if s.kind.startswith("ffn") else act_attention)(act, s)

        def pe_transposes(pe, s, then):
            for g in range(NB):
                pe.wait_ge(s.xn_ready, g + 1)
                if g >= 2:
                    pe.wait_ge(s.tr_evac, g - 1)
                for t in range(TPB):
                    mm = nc.tensor.transpose(ps[:, g % 2, t * P:(t + 1) * P], xn[:, g * TPB + t, :], ident)
                mm.then_inc(s.tr_done, 1)
                if g >= 1:
                    then(g - 1)
            then(NB - 1)

        def pe_ffn(pe, s):
            L = int(s.kind[3])

            def logits(g):
                pe.wait_ge(s.tr_evac, g + 1)
                for t in range(g * TPB, (g + 1) * TPB):
                    mm = nc.tensor.matmul(ps[:, 6, t * E:(t + 1) * E], xnT[:, t * P:(t + 1) * P], rw[L][:],
                                          start=True, stop=True)
                mm.then_inc(s.lg_done, 1)

            pe_transposes(pe, s, logits)
            if L == 1:
                pe.wait_ge(s.sel_ready, 1)
                sel = sel_bf[:].rearrange("p t e -> p (t e)")
                nc.tensor.matmul(ps[:, 6, 0:NT * E], tri_bf, sel, start=True, stop=True)
                nc.tensor.matmul(ps[:, 7, 0:NT * E], ones_bf[:], sel, start=True, stop=True).then_inc(s.cnt_done, 1)
            pe.sem_inc(s.down_done, 2)
            pe.wait_ge(w_in, 16 * 2 * s.loads)

            def up(j, e):
                for c in range(NC):
                    pe.wait_ge(s.gelu_done, (j * E + e) * NC + c + 1)
                    nc.tensor.matmul(ps[:, c, :], w1[:, e, c * P:(c + 1) * P], xnT[:, bass.ds(j * BLK, BLK)],
                                     start=True, stop=True).then_inc(s.tr_done, 1)

            def down(j, e):
                pe.wait_ge(s.gelu_done, (j * E + e) * NC + NC + 4)
                pe.wait_ge(s.comb_done, j * E + e + 1)
                y = ps[:, 4 + e % 2, :]
                if L == 0:
                    for a in range(PARTS):
                        nc.tensor.matmul(y.rearrange("p (t d) -> p t d", d=D), ones_bf[0:1, :],
                                         bcast(b2p[:, a, e * D:(e + 1) * D], 1, TPB),
                                         start=(a == 0), stop=False, skip_group_check=True)
                for t in range(TPB):
                    for c in range(NC):
                        mm = nc.tensor.matmul(y[:, t * D:(t + 1) * D], hT[:, e % 2, c, t * P:(t + 1) * P],
                                              w2[:, e, c, :], start=(L == 1 and c == 0), stop=(c == NC - 1),
                                              skip_group_check=True)
                mm.then_inc(s.down_done, 1)

            with pe.Fori(0, NB) as j:
                up(j, 0)
                for e in range(E):
                    if e + 1 < E:
                        up(j, e + 1)
                    down(j, e)

        def pe_attention(pe, s):
            pe_transposes(pe, s, lambda g: None)
            xb = lambda j: xnT[:, j * BLK:(j + 1) * BLK]
            pe.wait_ge(s.tr_evac, NB)
            if s.kind == "attn0":
                for j in range(NB):
                    if j >= 1:
                        pe.wait_ge(s.qkv_free, 2 * j)
                    for w in range(4):
                        mm = nc.tensor.matmul(ps[:, w, :], wqkv[:, w, :], xb(j), start=True, stop=True)
                    mm.then_inc(s.qkv_done, 1)
            else:
                for j in range(NB):
                    if j >= 1:
                        pe.wait_ge(s.c_evac, 2 * j)
                    for w in range(2):
                        nc.tensor.matmul(ps[0:32, 4 + w, :], wd[:, w, :], xb(j), start=True,
                                         stop=True).then_inc(s.c_done, 1)
                    pe.wait_ge(s.c_evac, 2 * j + 2)
                    if j >= 1:
                        pe.wait_ge(s.qkv_free, 2 * j)
                    nc.tensor.matmul(ps[:, 0, :], wu[:, 0, :], cq[:], start=True, stop=True)
                    nc.tensor.matmul(ps[:, 2, :], wu[:, 1, :], ckv[:, j * BLK:(j + 1) * BLK], start=True,
                                     stop=True).then_inc(s.qkv_done, 1)
            for j in range(NB):
                if j >= 2:
                    pe.wait_ge(s.v_evac, 2 * j - 2)
                for t in range(TPB):
                    c = (j * TPB + t) * P
                    lhs, rhs = (xnT[:, c:c + P], wqkv[:, 4, :]) if s.kind == "attn0" else (ckv[:, c:c + P], wu[:, 2, :])
                    mm = nc.tensor.matmul(ps[:, 6 + j % 2, t * P:(t + 1) * P], lhs, rhs, start=True, stop=True)
                mm.then_inc(s.v_done, 1)
            pe.wait_ge(s.v_evac, 2 * NB)
            pe.wait_ge(s.qkv_free, 2 * NB)

            def head_max(i, r, m, q, c, w):
                n = i * RING + r
                if m == 0:
                    pe.wait_ge(s.qk_in[r], 16 * LOADS * (i + 1))
                    pe.wait_ge(s.msplit, n + 1)
                pe.wait_ge(s.red_done, n * s.M + m + 1)
                diag = s.causal and c + w == (q + 1) * P
                mm = nc.tensor.matmul(ps[:, 4 + m % 2, 0:w], qs[0:KQ, r, q * P:(q + 1) * P],
                                      ks[0:KQ, r, c:c + w], start=True, stop=not diag, skip_group_check=True)
                if diag:
                    mm = nc.tensor.matmul(ps[:, 4 + m % 2, w - P:w], ident_bf, maskS, start=False, stop=True,
                                          skip_group_check=True)
                mm.then_inc(s.sm_done, 1)

            def turn_max(i, r):
                n = i * RING + r
                pe.wait_ge(s.row_done, n + 1)
                nc.tensor.transpose(ps[0:NKT, 4, 0:P], rowmax[:, r, 0, :], ident).then_inc(s.mt_done, 1)

            def scores(i, r, g):
                n, (hf, kt) = i * RING + r, s.groups[g]
                if g == 0:
                    pe.wait_ge(s.m_in[r], 16 * PARTS * (i + 1))
                pe.wait_ge(s.exp_done, n * s.G + g + 1)
                for m in range(2):
                    off = kt + m - 4 * hf
                    diag = s.causal and off >= 0
                    lo = off * P if diag else 0
                    mm = nc.tensor.matmul(ps[:, 2 * (g % 2) + m, lo:BLK], ks[0:KS, r, (kt + m) * P:(kt + m + 1) * P],
                                          qs[0:KS, r, hf * BLK + lo:(hf + 1) * BLK], start=True, stop=not diag,
                                          skip_group_check=True)
                    if diag:
                        mm = nc.tensor.matmul(ps[:, 2 * (g % 2) + m, lo:lo + P], ident_bf, maskT, start=False,
                                              stop=True, skip_group_check=True)
                mm.then_inc(s.st_done, 1)

            def values(i, r, g):
                n, (hf, kt) = i * RING + r, s.groups[g]
                slot = (s.G * r + g) % W_RING
                pe.wait_ge(s.exp_done, n * s.G + g + 1 + 2)
                own, done = (s.on_dve, s.sub_dve) if g in s.on_dve else (s.on_pool, s.sub_pool)
                pe.wait_ge(done, n * len(own) + own.index(g) + 1)
                if g == 0:
                    pe.wait_ge(s.nrm_done, n + 1)
                for m in range(2):
                    off = kt + m - 4 * hf
                    for qt in range(max(0, off) if s.causal else 0, TPB):
                        end = kt + m == (4 * hf + qt if s.causal else NKT - 1)
                        for a in range(2):
                            q = hf * TPB + qt
                            mm = nc.tensor.matmul(ps[:, 6 + r % 2, q * VW:(q + 1) * VW],
                                                  wp[:, a, slot, m * BLK + qt * P:m * BLK + (qt + 1) * P],
                                                  vr[:, r, kt + m, :], start=(g == 0 and m == 0 and qt == 0 and a == 0),
                                                  stop=(end and a == 1), skip_group_check=True)
                mm.then_inc(s.pv_done, 1)

            def step(i, r, ahead):
                one, two = (i + (r + 1) // RING, (r + 1) % RING), (i + (r + 2) // RING, (r + 2) % RING)
                before = (i - 1, RING - 1) if r == 0 else (i, r - 1)
                for g in range(s.G):
                    scores(i, r, g)
                    if g == 0 and ahead >= 1:
                        turn_max(*one)
                    if g >= LAG:
                        values(i, r, g - LAG)
                    elif type(i) is not int or i or r:
                        values(*before, s.G + g - LAG)
                    if ahead >= 2:
                        for piece in s.pieces[g]:
                            head_max(*two, *piece)

            pe.sem_inc(s.pv_done, PV0)
            for piece in s.all_pieces:
                head_max(0, 0, *piece)
            turn_max(0, 0)
            for piece in s.all_pieces:
                head_max(0, 1, *piece)

            def loop(count):
                with pe.Fori(0, count) as i:
                    yield i

            rounds(loop, step)
            for g in range(s.G - LAG, s.G):
                values(HEADS // RING - 1, RING - 1, g)
            L = int(s.kind[4])
            def project(j):
                pe.wait_ge(s.at_evac, j + 1)
                if j >= 2:
                    pe.wait_ge(s.wo_free, j - 1)
                for t in range(TPB):
                    c = (j * TPB + t) * P
                    mm = nc.tensor.matmul(ps[:, 2 + j % 2, t * P:(t + 1) * P], xnT[:, c:c + P],
                                          wo[L][:], start=True, stop=True)
                mm.then_inc(s.wo_done, 1)

            pe.wait_ge(s.nrm_done, HEADS + 2)
            for j in range(NB):
                if j >= 2:
                    pe.wait_ge(s.at_evac, j - 1)
                for t in range(TPB):
                    mm = nc.tensor.transpose(ps[:, j % 2, t * P:(t + 1) * P], xn[:, j * TPB + t, :], ident)
                mm.then_inc(s.at_done, 1)
                if j >= 1:
                    project(j - 1)
            project(NB - 1)

        @block.tensor
        def _(pe):
            pe.wait_ge(c_ready, 1)
            for s in S:
                (pe_ffn if s.kind.startswith("ffn") else pe_attention)(pe, s)

        @block.gpsimd
        def _(pool):
            for s in S:
                if s.kind.startswith("attn"):
                    with pool.Fori(0, HEADS // RING) as i:
                        for r in range(RING):
                            for g in s.on_pool:
                                pool.wait_ge(s.exp_done, (i * RING + r) * s.G + g + 3)
                                subtract(nc.gpsimd, s, r, g, s.sub_pool)

        @block.vector
        def _(dve):
            st = Steps(dve, dve_step)
            link = st.link
            v = nc.vector
            dve.wait_ge(par_in, 16 * N_SMALL)
            link(v.memset(ones_bf[:], 1.0))
            link(v.tensor_copy(b2p[:, 0, :], b2f))
            link(v.tensor_tensor(b2r, b2f, b2p[:, 0, :], ALU.subtract))
            link(v.tensor_copy(b2p[:, 1, :], b2r))
            link(v.tensor_tensor(b2p[:, 2, :], b2r, b2p[:, 1, :], ALU.subtract))
            link(v.memset(vall[:, :, :, VW - 1:VW], 1.0))
            link(v.memset(ks[64:P, :, :], -1.0))
            link(v.tensor_copy(cbf[:], consts[:, 0:4 * P]))
            dve.sem_inc(c_ready, 1)
            dve.wait_ge(x_in, 16)

            def normalise():
                for g in range(4):
                    t = slice(g * 8, (g + 1) * 8)
                    link(v.tensor_reduce(mean[:, t], x[:, t, :], AX.X, ALU.add))
                    link(v.tensor_scalar(mean[:, t], mean[:, t], 1.0 / D, None, ALU.mult))
                    v.tensor_tensor(xn[:, t, :], x[:, t, :], bcast(mean[:, t], 2, D),
                                    ALU.subtract).then_inc(s.xc_ready, 1)
                for g in range(4):
                    dve.wait_ge(s.sq_ready, g + 1)
                    link(v.tensor_reduce(var[:, g * 8:(g + 1) * 8],
                                         xnT[:, g * 1024:(g + 1) * 1024].rearrange("p (t d) -> p t d", d=D),
                                         AX.X, ALU.add))
                v.tensor_scalar(var[:], var[:], 1.0 / D, 1e-5, ALU.mult, ALU.add).then_inc(s.std_in, 1)
                dve.wait_ge(s.std_ready, 1)
                inverse_root()
                for g in range(NB):
                    t = slice(g * TPB, (g + 1) * TPB)
                    v.tensor_tensor(xn[:, t, :], xn[:, t, :], bcast(rstd[:, t], 2, D),
                                    ALU.mult).then_inc(s.xn_ready, 1)

            def inverse_root():
                link(v.reciprocal(rstd[:], t32[:]))
                link(v.tensor_tensor(t32[:], rstd[:], rstd[:], ALU.mult))
                link(v.tensor_tensor(t32[:], t32[:], var[:], ALU.mult))
                link(v.tensor_scalar(t32[:], t32[:], -0.5, 1.5, ALU.mult, ALU.add))
                link(v.tensor_tensor(rstd[:], rstd[:], t32[:], ALU.mult))

            def first_of(dst, value, top):
                link(v.tensor_tensor(r2[:], value, bcast(top[:], 2, E), ALU.is_equal))
                link(v.tensor_tensor(r2[:], r2[:], bcast(first_pref, 1, NT), ALU.mult))
                link(v.tensor_reduce(pw1[:], r2[:], AX.X, ALU.max))
                link(v.tensor_tensor(dst, r2[:], bcast(pw1[:], 2, E), ALU.is_equal))

            def top_two(value):
                link(v.tensor_reduce(top1[:], value, AX.X, ALU.max))
                first_of(sel1[:], value, top1)
                link(v.scalar_tensor_tensor(value, sel1[:], -3e38, value, ALU.mult, ALU.add))
                link(v.tensor_reduce(top2[:], value, AX.X, ALU.max))
                first_of(sel2[:], value, top2)

            def route(s):
                dve.wait_ge(s.lg_done, NB)
                logits = ps[:, 6, 0:NT * E].rearrange("p (t e) -> p t e", e=E)
                if s.kind == "ffn0":
                    link(v.tensor_tensor(lg[:], logits, bcast(rb[:], 1, NT), ALU.add))
                    top_two(lg[:])
                    v.tensor_tensor(top2[:], top2[:], top1[:], ALU.subtract).then_inc(s.ex_in, 1)
                    dve.wait_ge(s.ex_ready, 1)
                    link(v.tensor_scalar(pw1[:], t32[:], 1.0, None, ALU.add))
                    link(v.reciprocal(pw1[:], pw1[:]))
                    link(v.tensor_tensor(pw2[:], pw1[:], t32[:], ALU.mult))
                else:
                    link(v.tensor_copy(lg[:], logits))
                    link(v.tensor_reduce(top1[:], lg[:], AX.X, ALU.max))
                    v.tensor_tensor(r1[:], lg[:], bcast(top1[:], 2, E), ALU.subtract).then_inc(s.ex_in, 1)
                    dve.wait_ge(s.ex_ready, 1)
                    link(v.tensor_reduce(t32[:], r1[:], AX.X, ALU.add))
                    link(v.reciprocal(t32[:], t32[:]))
                    link(v.tensor_tensor(r1[:], r1[:], bcast(t32[:], 2, E), ALU.mult))
                    top_two(r1[:])
                    link(v.tensor_copy(pw1[:], top1[:]))
                    link(v.tensor_copy(pw2[:], top2[:]))
                    v.tensor_tensor(sel_bf[:], sel1[:], sel2[:], ALU.add).then_inc(s.sel_ready, 1)
                    dve.wait_ge(s.cnt_done, 1)
                    tot = ps[:, 7, 0:NT * E].rearrange("p (t e) -> p t e", e=E)
                    a, b = r1, r2
                    link(v.memset(a[:, 0:1, :], 0.0))
                    link(v.tensor_copy(a[:, 1:NT, :], tot[:, 0:NT - 1, :]))
                    k = 1
                    while k < NT:
                        link(v.tensor_copy(b[:, 0:k, :], a[:, 0:k, :]))
                        link(v.tensor_tensor(b[:, k:NT, :], a[:, k:NT, :], a[:, 0:NT - k, :], ALU.add))
                        a, b = b, a
                        k *= 2
                    link(v.tensor_tensor(lg[:], ps[:, 6, 0:NT * E].rearrange("p (t e) -> p t e", e=E), a[:], ALU.add))
                    link(v.tensor_scalar(lg[:], lg[:], float(CAPACITY), None, ALU.is_lt))
                link(v.tensor_tensor(sel1[:], sel1[:], bcast(pw1[:], 2, E), ALU.mult))
                link(v.tensor_tensor(sel2[:], sel2[:], bcast(pw2[:], 2, E), ALU.mult))
                link(v.tensor_tensor(cw[:], sel1[:], sel2[:], ALU.add))
                if s.kind == "ffn1":
                    link(v.tensor_tensor(cw[:], cw[:], lg[:], ALU.mult))

            def ffn(s):
                normalise()
                route(s)
                first = s.kind == "ffn0"
                dve.sem_inc(s.comb_done, 2)
                for j in st.loop(NB, 8 if first else 3):
                    tiles = bass.ds(j * TPB, TPB)
                    link(v.tensor_scalar(cwb[:], cw[:, tiles, :], 1.0, None, ALU.mult))
                    link(v.tensor_scalar(acc[:], xn[:, tiles, :] if first else bcast(ffn_bias[:], 1, TPB), 1.0, None,
                                         ALU.mult))
                    for e in range(E):
                        dve.wait_ge(s.down_done, j * E + e + 3)
                        dve.wait_ge(s.comb_done, j * E + e + 2)
                        for t in range(TPB):
                            ins_ = v.scalar_tensor_tensor(acc[:, t, :], ps[:, 4 + e % 2, t * D:(t + 1) * D],
                                                          cwb[:, t, e:e + 1], acc[:, t, :], ALU.mult, ALU.add)
                        ins_.then_inc(s.comb_done, 1)
                    dve.wait_ge(s.comb_done, j * E + E + 2)
                    if first:
                        link(v.tensor_reduce(cwb[:, :, 0], acc[:], AX.X, ALU.add))
                        link(v.tensor_scalar(cwb[:, :, 0], cwb[:, :, 0], 1.0 / D, None, ALU.mult))
                        link(v.tensor_tensor(acc[:], acc[:], cwb[:, :, 0:1].to_broadcast([P, TPB, D]), ALU.subtract))
                        link(v.tensor_scalar(xn[:, tiles, :], acc[:], 1.0, None, ALU.mult))
                        link(v.tensor_tensor(sq[:], acc[:], acc[:], ALU.mult))
                        link(v.tensor_reduce(var[:, tiles], sq[:], AX.X, ALU.add))
                    else:
                        link(v.scalar_tensor_tensor(x[:, tiles, :], acc[:], 0.5, x[:, tiles, :], ALU.mult, ALU.add))
                if first:
                    link(v.tensor_scalar(var[:], var[:], 1.0 / D, 1e-12, ALU.mult, ALU.add))
                    v.tensor_copy(var[:], var[:]).then_inc(s.std_in, 1)
                    dve.wait_ge(s.std_ready, 2)
                    inverse_root()
                    link(v.tensor_tensor(xn[:], xn[:], bcast(rstd[:], 2, D), ALU.mult))
                    link(v.tensor_tensor(xn[:], xn[:], bcast(lnw[:], 1, NT), ALU.mult))
                    link(v.tensor_tensor(xn[:], xn[:], bcast(lnb[:], 1, NT), ALU.add))
                    link(v.scalar_tensor_tensor(x[:], xn[:], 0.5, x[:], ALU.mult, ALU.add))

            def split(s, j, w):
                f, rest = qk_f[:, 2 + 2 * w, :], qk_f[:, 3 + 2 * w, :]
                m = 2 * j + w
                dve.wait_ge(s.p_copied, 2 * m + 1)
                v.tensor_tensor(rest, f, parts[:, w, 0, :], ALU.subtract).then_inc(s.r_ready, 1)
                dve.wait_ge(s.r_ready, 2 * m + 2)
                dve.wait_ge(s.p_copied, 2 * m + 2)
                v.tensor_tensor(parts[:, w, 2, :], rest, parts[:, w, 1, :], ALU.subtract).then_inc(s.parts_ready, 1)

            def attention(s):
                normalise()
                rope = s.kind == "attn0"
                for j in range(NB):
                    pos = slice((j % 2) * BLK, (j % 2) * BLK + BLK)
                    for w in range(2):
                        dve.wait_ge(s.qkv_done, j + 1)
                        if j >= 1:
                            dve.wait_ge(s.parts_ready, 2 * (j - 1) + w + 1)
                        if rope:
                            link(v.scalar_tensor_tensor(qk_f[:, 0, :], ps[:, 2 * w, :], bqk[:, 2 * w:2 * w + 1],
                                                        trig[:, 0, pos], ALU.add, ALU.mult))
                            ins_ = v.scalar_tensor_tensor(qk_f[:, 1, :], ps[:, 2 * w + 1, :],
                                                          bqk[:, 2 * w + 1:2 * w + 2], trig[:, 1, pos],
                                                          ALU.add, ALU.mult)
                            ins_.then_inc(s.qkv_free, 1)
                            dve.wait_ge(s.qkv_free, 2 * j + w + 1)
                            v.tensor_tensor(qk_f[:, 2 + 2 * w, :], qk_f[:, 0, :], qk_f[:, 1, :],
                                            ALU.add).then_inc(s.r_ready, 1)
                        else:
                            link(v.tensor_copy(qk_f[:, 2 + 2 * w, :], ps[:, 2 * w, :]))
                            dve.sem_inc(s.qkv_free, 1)
                            dve.sem_inc(s.r_ready, 1)
                        dve.wait_ge(s.r_ready, 4 * j + 2 * w + 1)
                        split(s, j, w)
                for j in range(NB):
                    b, k0 = j // 2, (j % 2) * TPB
                    dst = [vall[:, b * H:(b + 1) * H, k0:k0 + TPB, a * DH:(a + 1) * DH].rearrange("p h k d -> p k h d")
                           for a in range(PARTS)]

                    def heads(ap):
                        return ap.rearrange("p (k h d) -> p k h d", k=TPB, h=H)

                    vf, rest = heads(qk_f[:, 0, :]), heads(qk_f[:, 1, :])
                    dve.wait_ge(s.v_done, j + 1)
                    if rope:
                        ins_ = v.tensor_tensor(qk_f[:, 0, :].rearrange("p (k c) -> p k c", k=TPB),
                                               ps[:, 6 + j % 2, :].rearrange("p (k c) -> p k c", k=TPB),
                                               bcast(bv[:], 1, TPB), ALU.add)
                    else:
                        ins_ = v.tensor_copy(qk_f[:, 0, :], ps[:, 6 + j % 2, :])
                    ins_.then_inc(s.v_evac, 1)
                    dve.wait_ge(s.v_evac, 2 * j + 1)
                    link(v.tensor_copy(dst[0], vf))
                    link(v.tensor_tensor(rest, vf, dst[0], ALU.subtract))
                    link(v.tensor_copy(dst[1], rest))
                    v.tensor_tensor(dst[2], rest, dst[1], ALU.subtract).then_inc(s.v_evac, 1)
                    dve.wait_ge(s.v_evac, 2 * j + 2)

                def reduce(i, r, m, q, c, w):
                    n = i * RING + r
                    dve.wait_ge(s.sm_done, n * s.M + m + 1)
                    v.tensor_reduce(rowmax[:, r, c // BLK, q:q + 1], ps[:, 4 + m % 2, 0:w], AX.X,
                                    ALU.max).then_inc(s.red_done, 1)
                    if m == s.M - 1:
                        q0 = NKT // 2 if s.causal else 0
                        dve.wait_ge(s.red_done, (n + 1) * s.M + 2)
                        v.tensor_tensor(rowmax[:, r, 0, q0:], rowmax[:, r, 0, q0:], rowmax[:, r, 1, q0:],
                                        ALU.max).then_inc(s.row_done, 1)

                def split_max(i, r):
                    n = i * RING + r
                    dve.wait_ge(s.mt_done, n + 1)
                    link(v.tensor_scalar(mf[:, 0, :], ps[0:NKT, 4, 0:P], -SHIFT / s.scale, None, ALU.add))
                    link(v.tensor_copy(mp[:, r, 0, :], mf[:, 0, :]))
                    link(v.tensor_tensor(mf[:, 1, :], mf[:, 0, :], mp[:, r, 0, :], ALU.subtract))
                    link(v.tensor_copy(mp[:, r, 1, :], mf[:, 1, :]))
                    v.tensor_tensor(mp[:, r, 2, :], mf[:, 1, :], mp[:, r, 1, :], ALU.subtract).then_inc(s.msplit, 1)

                def sub(i, r, g):
                    dve.wait_ge(s.exp_done, (i * RING + r) * s.G + g + 3)
                    subtract(v, s, r, g, s.sub_dve)

                def divide(i, r):
                    n = i * RING + r
                    o = ps[:, 6 + r % 2, 0:NKT * VW].rearrange("p (q c) -> p q c", c=VW)
                    tiles = bass.ds((i // (H // RING)) * NKT, NKT)
                    head = bass.ds((i % (H // RING)) * RING * DH + r * DH, DH)
                    dve.wait_ge(s.pv_done, PV0 + (n + 1) * s.G)
                    link(v.reciprocal(rec[:], o[:, :, VW - 1]))
                    link(v.tensor_reduce(osum[:], o[:, :, 0:PARTS * DH].rearrange("p q (a d) -> p q d a", a=PARTS),
                                         AX.X, ALU.add))
                    v.tensor_tensor(xn[:, tiles, head], osum[:], bcast(rec[:], 2, DH), ALU.mult).then_inc(s.nrm_done, 1)

                def step(i, r, ahead):
                    one, two = (i + (r + 1) // RING, (r + 1) % RING), (i + (r + 2) // RING, (r + 2) % RING)
                    if ahead >= 1:
                        split_max(*one)
                    before = (i - 1, RING - 1) if r == 0 else (i, r - 1)
                    for g in range(s.G):
                        if ahead >= 2:
                            for piece in s.pieces[g]:
                                reduce(*two, *piece)
                        if g in s.on_dve:
                            sub(i, r, g)
                        if g == LAG and (type(i) is not int or i or r):
                            divide(*before)

                dve.sem_inc(s.nrm_done, 2)
                dve.sem_inc(s.msplit, 1)
                dve.sem_inc(s.red_done, 2)
                for piece in s.all_pieces:
                    reduce(0, 0, *piece)
                split_max(0, 0)
                for piece in s.all_pieces:
                    reduce(0, 1, *piece)
                rounds(lambda count: st.loop(count, 6 * RING), step)
                divide(HEADS // RING - 1, RING - 1)
                for j in range(NB):
                    dve.wait_ge(s.wo_done, j + 1)
                    t = slice(j * TPB, (j + 1) * TPB)
                    src = ps[:, 2 + j % 2, :].rearrange("p (t d) -> p t d", d=D)
                    if rope:
                        link(v.tensor_tensor(x[:, t, :], x[:, t, :], bcast(bo[:], 1, TPB), ALU.add))
                    v.tensor_tensor(x[:, t, :], src, x[:, t, :], ALU.add).then_inc(s.wo_free, 1)
                dve.wait_ge(s.wo_free, NB)

            for s in S:
                (ffn if s.kind.startswith("ffn") else attention)(s)
                dve.sem_inc(stage_done, 1)


N_SMALL = 18
STAGES = ("ffn0", "attn0", "ffn0", "ffn1", "attn1", "ffn1")


def constants():
    p, c = np.arange(P)[:, None], np.arange(P)[None, :]
    consts = np.zeros((P, CONST_COLS), np.float32)
    consts[:, 0:P] = p == c
    consts[:, P:2 * P] = p < c
    consts[:, 2 * P:3 * P] = np.where(c > p, NEG, 0)
    consts[:, 3 * P:4 * P] = np.where(p > c, NEG, 0)
    consts[:, 4 * P:] = E - np.arange(E)[None, :]
    inv = (1.0 / np.float32(10000.0) ** (np.arange(0, DH, 2, dtype=np.float32) / np.float32(DH))).astype(np.float32)
    ang = np.repeat(np.arange(N, dtype=np.float32)[:, None] * inv[None, :], 2, axis=-1)
    sign = np.where(np.arange(DH) % 2 == 0, -1.0, 1.0).astype(np.float32)
    cos, sin = np.cos(ang).astype(np.float32), (np.sin(ang) * sign).astype(np.float32)
    trig = np.stack([np.tile(cos.T, (H, 1)), np.tile(sin.T, (H, 1))], axis=1)
    return consts, np.ascontiguousarray(trig)


def kernel(**inputs):
    import concourse.bacc as bacc
    from concourse.bass_utils import run_bass_kernel_spmd as run

    a = {k: np.asarray(v) for k, v in inputs.items()}
    swap = np.arange(D) ^ 1
    consts, trig = constants()
    wq, wk, wv = (a[f"L0_attn_W{k}"] for k in "qkv")
    bq, bk = a["L0_attn_bq"], a["L0_attn_bk"]
    arrays = {
        "x": a["L0_attn_x"].reshape(T, D),
        "consts": consts,
        "trig": trig,
        "rb": a["L0_ffn_router_b"],
        "rw0": a["L0_ffn_router_w"].T,
        "rw1": a["L1_ffn_w_router"],
        "b1": a["L0_ffn_b1"].reshape(E, NC, P).transpose(2, 0, 1),
        "b2": a["L0_ffn_b2"].reshape(1, E * D),
        "lnw": a["L0_ffn_ln_w"],
        "lnb": a["L0_ffn_ln_b"],
        "ffn_bias": a["L1_ffn_bias"].reshape(D),
        "w1_0": a["L0_ffn_w1"].transpose(2, 0, 1),
        "w2_0": a["L0_ffn_w2"].reshape(E, D, NC, P).transpose(3, 0, 2, 1),
        "w1_1": a["L1_ffn_w1"].transpose(1, 0, 2),
        "w2_1": a["L1_ffn_w2"].reshape(E, NC, P, D).transpose(2, 0, 1, 3),
        "wqkv": np.stack([wq, wq[:, swap], wk, wk[:, swap], wv], axis=1),
        "bqk": np.stack([bq, bq[swap], bk, bk[swap]], axis=1),
        "bv": a["L0_attn_bv"],
        "bo": a["L0_attn_bo"],
        "wo0": a["L0_attn_Wo"],
        "wo1": a["L1_attn_W_o"],
        "wd": np.stack([a["L1_attn_W_dq"], a["L1_attn_W_dkv"]], axis=1),
        "wu": np.stack([a["L1_attn_W_uq"], a["L1_attn_W_uk"], a["L1_attn_W_uv"]], axis=1),
    }
    nc = bacc.Bacc("TRN2", target_bir_lowering=False, num_devices=1)
    maps, ins = {}, {}
    for name, v in arrays.items():
        v = np.ascontiguousarray(v)
        maps[f"in_{name}"] = v
        ins[name] = nc.dram_tensor(f"in_{name}", v.shape, mybir.dt.from_np(v.dtype), kind="ExternalInput").ap()
    out = nc.dram_tensor("out", (T, D), F32, kind="ExternalOutput").ap()
    build(nc, ins, out, STAGES)
    r = run(nc, [maps], core_ids=[0])
    return r.results[0]["out"].reshape(B, N, D)
```

```python
from contextlib import ExitStack

import numpy as np
import concourse.bass as bass
from concourse import mybir
from concourse.alu_op_type import AluOpType as ALU

F32, BF16, F16, I32 = mybir.dt.float32, mybir.dt.bfloat16, mybir.dt.float16, mybir.dt.int32
ACT, AX = mybir.ActivationFunctionType, mybir.AxisListType
P = 128
B, N, D = 4, 1024, 128
T = B * N
NT = T // P
BLK = 512
NB = T // BLK
TPB = BLK // P
E, FF = 8, 512
NC = FF // P
CAPACITY = 2 * T // E
TS = 256
TILES = (-(-(2 * T + E * (TS - 1)) // (TS * 4)) * 4, E * CAPACITY // TS)
SLOTS = max(TILES) * TS
BODY = (4, 8)
SHARE = (1, CAPACITY // TS)
W_SLOTS = (4, 2)
X_RING = 4
O_W2, O_B1, O_B2 = FF, FF + NC * D, FF + NC * D + NC
W_COLS = O_B2 + D
H, DH = 16, 8
HEADS = B * H
NKT = N // P
PARTS = 3
KQ = PARTS * PARTS * DH
KM = 96
VW = PARTS * DH + 1
SHIFT = 10.0
TURNED = 256
LAG = 2
W_RING = 4
RING = 4
EXP_ROUND = 16
NEG = -1e30
HALVES = SLOTS // P
NO_ROOM = float(2 * SLOTS)
CONST_COLS = 4 * P + 2 * E + TILES[0] + P + 2 * HALVES + 2 * NT
HOT_CHUNKS = 4
LOADS = 2 + PARTS
POOL_GROUPS = ((1, 3, 5, 6, 7), (1, 3, 5))
SIDE_STEPS = ((3, 1, 4), (2, 1, 1))


class Steps:

    def __init__(self, engine, sem):
        self.engine, self.sem, self.n, self.base = engine, sem, 0, 0

    def link(self, instruction):
        instruction.then_inc(self.sem, 1)
        self.n += 1
        self.engine.wait_ge(self.sem, self.base + self.n)

    def loop(self, count, per):
        start = self.n
        with self.engine.Fori(0, count) as i:
            self.base = i * per
            yield i
            assert self.n - start == per, (self.n - start, per)
        self.base, self.n = 0, start + count * per


def rounds(engine_loop, step):
    last = HEADS // RING - 1
    step(0, 0, 2)
    for i in engine_loop(last):
        for r in range(1, RING):
            step(i, r, 2)
        step(i + 1, 0, 2)
    for r in range(1, RING):
        step(last, r, min(2, RING - 1 - r))


class Stage:

    def __init__(self, sem, shared, k, stages):
        def new(name):
            return sem(f"{name}_{k}")

        self.k, self.kind = k, stages[k]
        self.ffns = len([q for q in stages[:k] if q.startswith("ffn")])
        self.xc_ready = shared["xc_ready"]
        self.sq_ready = shared["sq_ready"]
        self.std_in = new("std_in")
        self.std_ready = new("std_ready")
        self.xn_ready = shared["xn_ready"]
        self.tr_done = shared["tr_done"]
        self.tr_evac = shared["tr_evac"]
        if self.kind.startswith("ffn"):
            self.lg_done = shared["lg_done"]
            self.ex_in = shared["ex_in"]
            self.ex_ready = shared["ex_ready"]
            self.sel_ready = shared["sel_ready"]
            self.cnt_done = shared["cnt_done"]
            self.map_ready = shared["map_ready"]
            self.hot_ready = shared["hot_ready"]
            self.tab_done = shared["tab_done"]
            self.idx_ready = shared["idx_ready"]
            self.tp_done = new("tp_done")
            self.xt_evac = new("xt_evac")
            self.up_done = new("up_done")
            self.gelu_done = new("gelu_done")
            self.down_done = new("down_done")
            self.y_ready = new("y_ready")
            self.z_ready = new("z_ready")
            self.z_sq = new("z_sq")
            self.L = L = int(self.kind[3])
            self.tiles, self.body, self.share, self.w_slots = TILES[L], BODY[L], SHARE[L], W_SLOTS[L]
            before = [int(q[3]) for q in stages[:k] if q.startswith("ffn")]
            self.ring0 = sum(TILES[q] // X_RING for q in before)
            self.w0 = [sum(TILES[q] // SHARE[q] // W_SLOTS[q] for q in before if w < W_SLOTS[q])
                       for w in range(max(W_SLOTS))]
        else:
            self.qkv_done = new("qkv_done")
            self.qkv_free = new("qkv_free")
            self.p_copied = new("p_copied")
            self.r_ready = new("r_ready")
            self.parts_ready = new("parts_ready")
            self.v_done = new("v_done")
            self.v_evac = new("v_evac")
            self.c_done = new("c_done")
            self.c_evac = new("c_evac")
            self.st_done = new("st_done")
            self.exp_done = new("exp_done")
            self.pv_done = new("pv_done")
            self.sm_done = new("sm_done")
            self.red_done = new("red_done")
            self.row_done = new("row_done")
            self.mt_done = new("mt_done")
            self.msplit = new("msplit")
            self.pool_step = new("pool_step")
            self.mf_ready = new("mf_ready")
            self.nrm_done = new("nrm_done")
            self.sub_dve = new("sub_dve")
            self.sub_pool = new("sub_pool")
            self.at_done = new("at_done")
            self.at_evac = new("at_evac")
            self.wo_done = new("wo_done")
            self.wo_free = new("wo_free")
            self.parts_out = [new(f"parts_out{r}") for r in range(2)]
            self.qk_in = [new(f"qk_in{r}") for r in range(RING)]
            self.m_in = [new(f"m_in{r}") for r in range(RING)]
            self.scale = float(1 / np.sqrt(np.float32(D if self.kind == "attn0" else DH)))
            self.causal = self.kind == "attn1"
            self.divide_at, self.fetch_at, self.split_at = SIDE_STEPS[self.causal]
            self.groups = [(hf, kt) for hf in range(2) for kt in range(0, NKT, 2)
                           if not (self.causal and kt >= 4 * (hf + 1))]
            self.G = len(self.groups)
            self.on_pool = POOL_GROUPS[self.causal]
            self.on_dve = tuple(g for g in range(self.G) if g not in self.on_pool)
            tiles = ((0, 1, 2), (3,), (4,), (5,), (6,), (7,)) if self.causal else tuple((q,) for q in range(NKT))
            self.pieces, m = [], 0
            for qs in tiles:
                own = []
                for q in qs:
                    keys = (q + 1) * P if self.causal else N
                    for c in range(0, keys, BLK):
                        own.append((m, q, c, min(BLK, keys - c)))
                        m += 1
                self.pieces.append(own)
            self.all_pieces = [p for own in self.pieces for p in own]
            self.M = m


def bodies(loop, count, step):
    step(0, True, False)
    for i in loop(count - 2):
        step(i + 1, False, False)
    step(count - 1, False, True)


def engine_loop(engine):
    def loop(count):
        with engine.Fori(0, count) as i:
            yield i
    return loop


def bcast(ap, axis, n):
    a = ap.unsqueeze(axis)
    shape = list(a.shape)
    shape[axis] = n
    return a.to_broadcast(shape)


def build(nc, ins, out, stages):
    with ExitStack() as ctx:
        def sb(name, shape, dt=F32):
            return ctx.enter_context(nc.sbuf_tensor(name, shape, dt))

        def sem(name):
            return ctx.enter_context(nc.semaphore(name))

        x = sb("x", [P, NT, D])
        xn = sb("xn", [P, NT, D])
        xnT = sb("xnT", [P, T])
        rw = [sb(f"rw_{k}", [P, E]) for k in range(2)]
        rb = sb("rb", [P, E])
        ffn_bias = sb("ffn_bias", [P, D])
        lnw, lnb = sb("lnw", [P, D]), sb("lnb", [P, D])
        consts = sb("consts", [P, CONST_COLS])
        ident = consts[:, 0:P]
        first_pref = consts[:, 4 * P:4 * P + E]
        expert_base = consts[:, 4 * P + E:4 * P + 2 * E]
        tile_start = consts[:, 4 * P + 2 * E:4 * P + 2 * E + TILES[0]]
        o = 4 * P + 2 * E + TILES[0]
        count_up = consts[:, o:o + P]
        lane_t = sb("lane_t", [P, 1])
        half_start = consts[:, o + P:o + P + HALVES]
        spare_row = consts[:, o + P + HALVES:o + P + 2 * HALVES]
        group_no = consts[:, o + P + 2 * HALVES:CONST_COLS]
        cbf = sb("cbf", [P, 4 * P], BF16)
        ident_bf, tri_bf, maskS, maskT = (cbf[:, k * P:(k + 1) * P] for k in range(4))
        ones_bf = sb("ones_bf", [P, P], BF16)
        mean, var, rstd, t32 = (sb(n, [P, NT]) for n in ("mean", "var", "rstd", "t32"))
        work = sb("work", [P, 8192])
        work_bf = work[:].bitcast(BF16)
        lg, r1, r2, sel1, sel2 = (sb(n, [P, NT, E]) for n in ("lg", "r1", "r2", "sel1", "sel2"))
        top1, top2, pw1, pw2 = (sb(n, [P, NT]) for n in ("top1", "top2", "pw1", "pw2"))
        sel_bf = sb("sel_bf", [P, NT, E], BF16)
        room, slot_f = sb("room", [P, 2, NT]), sb("slot_f", [P, 2, NT])
        place, half = sb("place", [P, 2 * NT]), sb("half", [P, 2 * NT])
        hot_place = xnT[:].bitcast(BF16).rearrange("p (g c) -> p g c", c=P)
        hot_half = work_bf[:, 0:4 * NT * HALVES].rearrange("p (g a c) -> p g a c", a=2, c=HALVES)
        hot_one = work_bf[:, 4 * NT * HALVES:6 * NT * HALVES].rearrange("p (g c) -> p g c", c=HALVES)
        lane = lane_t[:, 0:1]
        slot_i = sb("slot_i", [P, 2 * NT], I32)
        used, late, row_f, tok_f = (sb(n, [P, HALVES]) for n in ("used", "late", "row_f", "tok_f"))
        token_of, row_of = sb("token_of", [P, HALVES], I32), sb("row_of", [P, HALVES], I32)
        total, n_tiles, ends, ends2, base = (sb(n, [P, E]) for n in ("total", "n_tiles", "ends", "ends2", "base"))
        fit = sb("fit", [P, E, T // TS])
        tile_cmp = sb("tile_cmp", [1, TILES[0], E])
        tile_f, tile_expert = sb("tile_f", [1, TILES[0]]), sb("tile_expert", [1, TILES[0]], I32)
        stat = sb("stat", [P, TPB])
        wts = sb("wts", [P, max(W_SLOTS), W_COLS])
        hT = work[:, 0:2 * NC * TS].rearrange("p (s c t) -> p s c t", s=2, c=NC)
        xt = work[:, 2048:2048 + 2 * TS].rearrange("p (s t) -> p s t", s=2)
        xs = work[:, 3072:3072 + X_RING * 2 * D].rearrange("p (s h d) -> p s h d", s=X_RING, h=2)
        ys = work[:, 4096:4096 + X_RING * 2 * D].rearrange("p (s h d) -> p s h d", s=X_RING, h=2)
        both = work[:].rearrange("p (t k d) -> p t k d", t=NT, k=2)
        z = xn

        def z_squares(j):
            return xnT[:, j * BLK:(j + 1) * BLK].rearrange("p (t d) -> p t d", d=D)

        ws = work[:, 0:4096].rearrange("p (s c) -> p s c", s=W_RING)
        wp = work[:, 4096:8192].bitcast(F16).rearrange("p (a s c) -> p a s c", a=2, s=W_RING)
        qk_f = work[:, 4096:8192].rearrange("p (k t) -> p k t", k=8)
        trig = sb("trig", [P, 2, N])
        wqkv = sb("wqkv", [P, 5, D])
        bqk = sb("bqk", [P, 4])
        bv, bo, wo = sb("bv", [P, D]), sb("bo", [P, D]), [sb(f"wo_{k}", [P, D]) for k in range(2)]
        wd = sb("wd", [P, 2, 32])
        wu = sb("wu", [32, 3, D])
        parts = sb("parts", [P, 2, PARTS, BLK], BF16)
        vall = sb("vall", [P, HEADS, NKT, VW], BF16)
        qs = sb("qs", [P, RING, N], BF16)
        ks = sb("ks", [P, RING, N], BF16)
        vr = sb("vr", [P, RING, NKT, VW], BF16)
        rowmax = sb("rowmax", [P, RING, 2, NKT])
        mf = sb("mf", [NKT, 2, P])
        mrest, nil = sb("mrest", [NKT, P]), sb("nil", [NKT, P])
        mp = sb("mp", [NKT, RING, PARTS, P], BF16)
        osum = sb("osum", [P, NKT, DH])
        rec = sb("rec", [P, NKT])
        cq = sb("cq", [32, 2, BLK])
        ckv = xn[0:32, :, :].rearrange("p t d -> p (t d)")

        ps = ctx.enter_context(nc.psum_tensor("ps", [P, 8, BLK], F32))

        qp = nc.dram_tensor("q_parts", [HEADS, PARTS * DH, N], BF16).ap()
        kp = nc.dram_tensor("k_parts", [HEADS, PARTS * DH, N], BF16).ap()

        xd = nc.dram_tensor("tokens_in", [T, D], F32).ap()
        yd = nc.dram_tensor("results", [2 * T + SLOTS, D], F32).ap()

        x_in, par_in, out_done = sem("x_in"), sem("par_in"), sem("out_done")
        w_in = [sem(f"w_in{w}") for w in range(max(W_SLOTS))]
        xd_out = sem("xd_out")
        xs_in = [sem(f"xs_in{r}") for r in range(X_RING)]
        y_out = [sem(f"y_out{r}") for r in range(X_RING)]
        gathered = [sem(f"gathered{j}") for j in range(NB)]
        c_ready = sem("c_ready")
        dve_step = sem("dve_step")
        stage_done = sem("stage_done")

        shared = {n: sem(n) for n in ("xc_ready", "sq_ready", "xn_ready", "tr_done", "tr_evac", "lg_done", "ex_in",
                                      "ex_ready", "sel_ready", "cnt_done", "map_ready", "hot_ready", "tab_done",
                                      "idx_ready")}
        S = [Stage(sem, shared, k, stages) for k in range(len(stages))]

        block = ctx.enter_context(nc.Block())

        def qkv_bank(s, j, w):
            return 4 * ((j + 1) % 2) + w if s.kind == "attn0" else w + j % 2

        PV0 = 8 * RING

        def spans(s, hf, kt):
            lo = [max(0, kt + m - 4 * hf) * P if s.causal else 0 for m in range(2)]
            return [(0, 0, 2)] if lo == [0, 0] else [(0, lo[0], 1), (1, lo[1], 1)]

        def span_of(tile, m, lo, w):
            return tile.rearrange("p (k q) -> p k q", k=2)[:, m:m + w, lo:BLK]

        def subtract(engine, s, r, g, done):
            slot = (s.G * r + g) % W_RING
            for m, lo, w in spans(s, *s.groups[g]):
                last = engine.tensor_tensor(span_of(wp[:, 1, slot, :], m, lo, w), span_of(ws[:, slot, :], m, lo, w),
                                            span_of(wp[:, 0, slot, :], m, lo, w), ALU.subtract)
            last.then_inc(done, 1)

        def sp_attention(sp, s):
            for j in range(NB):
                b, c0 = j // 2, (j % 2) * BLK
                for w, dst in ((0, qp), (1, kp)):
                    sp.wait_ge(s.parts_ready, 2 * j + w + 1)
                    d = dst[b * H:(b + 1) * H, :, c0:c0 + BLK].rearrange("h (a d) t -> a h d t", a=PARTS)
                    for a in range(PARTS):
                        sp.dma_start(d[a], parts[:, w, a, :]).then_inc(s.parts_out[w], 16)
            for w in range(2):
                sp.wait_ge(s.parts_out[w], 16 * NB * PARTS)

            def load(i, r, waits):
                n = i * RING + r
                q_src = qp[bass.ds(n, 1), :, :].rearrange("o p t -> (o p) t")
                k_src = [kp[bass.ds(n, 1), a * DH:(a + 1) * DH, :].rearrange("o p t -> (o p) t")
                         for a in range(PARTS)]
                v_src = vall[:, bass.ds(n, 1), :, :].rearrange("p o k d -> p (o k) d")
                if waits is not None:
                    sp.wait_ge(s.pv_done, waits)
                sp.dma_start(qs[0:KQ, r, :], bcast(q_src, 0, PARTS)).then_inc(s.qk_in[r], 16)
                for a in range(PARTS):
                    sp.dma_start(ks[a * 24:(a + 1) * 24, r, :], bcast(k_src[a], 0, PARTS)).then_inc(s.qk_in[r], 16)
                sp.dma_start(vr[:, r, :, :], v_src).then_inc(s.qk_in[r], 16)

            def max_rows(i, r):
                sp.wait_ge(s.msplit, i * RING + r + 3)
                for a in range(PARTS):
                    sp.dma_start(qs[KM + a:KM + a + 1, r, :].rearrange("o (q c) -> o q c", c=P),
                                 mp[:, r, a, :]).then_inc(s.m_in[r], 16)

            def step(i, r, ahead, more):
                if ahead:
                    max_rows(i + (r + 1) // RING, (r + 1) % RING)
                if more:
                    load(i + 1, r, PV0 + s.G * (i * RING + r + 1))

            sp.wait_ge(s.v_evac, 2 * NB)
            for r in range(RING):
                load(0, r, None)
            max_rows(0, 0)
            with sp.Fori(0, HEADS // RING - 1) as i:
                for r in range(RING):
                    step(i, r, True, True)
            for r in range(RING):
                step(HEADS // RING - 1, r, r + 1 < RING, False)

        def sp_ffn(sp, s):
            src = ins[f"experts{s.L}"]

            def weights(n, w):
                if s.L == 0:
                    n = sp.value_load(tile_expert[0:1, bass.ds(n, 1)], min_val=0, max_val=E - 1)
                cols = src.shape[2]
                sp.dma_start(wts[:, w, 0:cols],
                             src[bass.ds(n, 1), :, :].rearrange("o p c -> (o p) c")).then_inc(w_in[w], 16)

            if s.k:
                sp.wait_ge(stage_done, s.k)
            sp.wait_ge(s.xn_ready, NB * (s.k + 1))
            sp.dma_start(xd.rearrange("(t p) d -> p t d", p=P), xn[:]).then_inc(xd_out, 16)
            if s.L == 0:
                sp.wait_ge(s.map_ready, s.ffns + 1)
            for w in range(s.w_slots):
                weights(w, w)

            def body(i, first, last):
                if last:
                    return
                for q in range(s.share - 1, s.body, s.share):
                    n, w = i * (s.body // s.share) + q // s.share, (q // s.share) % s.w_slots
                    sp.wait_ge(s.y_ready, i * s.body + q + 1)
                    weights(n + s.w_slots, w)

            bodies(engine_loop(sp), s.tiles // s.body, body)
            for r in range(X_RING):
                sp.wait_ge(y_out[r], 32 * (s.ring0 + s.tiles // X_RING))
            for j in range(NB):
                for k in range(2):
                    rows = yd[k * T + j * BLK:k * T + (j + 1) * BLK, :].rearrange("(t p) d -> p t d", p=P)
                    sp.dma_start(both[:, j * TPB:(j + 1) * TPB, k, :], rows).then_inc(gathered[j], 16)

        @block.sync
        def _(sp):
            sp.dma_start(x[:], ins["x"].rearrange("(t p) d -> p t d", p=P)).then_inc(x_in, 16)
            small = [(consts[:], ins["consts"]), (rb[:], ins["rb"].partition_broadcast(P)),
                     (rw[0][:], ins["rw0"]), (rw[1][:], ins["rw1"]), (lnw[:], ins["lnw"].partition_broadcast(P)),
                     (lnb[:], ins["lnb"].partition_broadcast(P)),
                     (ffn_bias[:], ins["ffn_bias"].partition_broadcast(P)),
                     (trig[:], ins["trig"]), (wqkv[:], ins["wqkv"]), (bqk[:], ins["bqk"]),
                     (bv[:], ins["bv"].partition_broadcast(P)), (bo[:], ins["bo"].partition_broadcast(P)),
                     (wo[0][:], ins["wo0"]), (wo[1][:], ins["wo1"]), (wd[:], ins["wd"]), (wu[:], ins["wu"])]
            for dst, src in small:
                sp.dma_start(dst, src).then_inc(par_in, 16)
            assert len(small) == N_SMALL
            for s in S:
                (sp_ffn if s.kind.startswith("ffn") else sp_attention)(sp, s)
            sp.wait_ge(stage_done, len(S))
            sp.dma_start(out.rearrange("(t p) d -> p t d", p=P), x[:]).then_inc(out_done, 16)
            sp.wait_ge(out_done, 16)

        def act_norm(act, s):
            for g in range(4):
                act.wait_ge(s.xc_ready, 4 * s.k + g + 1)
                nc.scalar.activation(xnT[:, g * 1024:(g + 1) * 1024],
                                     xn[:, g * 8:(g + 1) * 8, :].rearrange("p t d -> p (t d)"),
                                     ACT.Square).then_inc(s.sq_ready, 1)
            act.wait_ge(s.std_in, 1)
            nc.scalar.activation(t32[:], var[:], ACT.Sqrt).then_inc(s.std_ready, 1)
            for g in range(NB):
                act.wait_ge(s.tr_done, NB * s.k + g + 1)
                nc.scalar.copy(xnT[:, g * BLK:(g + 1) * BLK], ps[:, g % 2, :]).then_inc(s.tr_evac, 1)

        def act_ffn(act, s):
            act_norm(act, s)
            zero = s.kind == "ffn0"
            act.wait_ge(s.ex_in, s.ffns + 1)
            if s.kind == "ffn0":
                nc.scalar.activation(t32[:], top2[:], ACT.Exp).then_inc(s.ex_ready, 1)
            else:
                nc.scalar.activation(r1[:], r1[:], ACT.Exp).then_inc(s.ex_ready, 1)

            def evacuate(t, q):
                act.wait_ge(s.tp_done, t + 1)
                nc.scalar.copy(xt[:, q % 2, :], ps[:, q % 2, 0:TS]).then_inc(s.xt_evac, 1)

            def body(i, first, last):
                for q in range(s.body):
                    t = i * s.body + q
                    act.wait_ge(s.up_done, t + 1)
                    if not first or q >= 2:
                        act.wait_ge(s.down_done, t - 1)
                    bank = 2 + 2 * (q % 2)
                    if zero:
                        for c in range(NC):
                            w = q % s.w_slots
                            last_ = nc.scalar.activation(hT[:, q % 2, c, :],
                                                         ps[:, bank + c // 2, c % 2 * TS:(c % 2 + 1) * TS], ACT.Gelu,
                                                         bias=wts[:, w, O_B1 + c:O_B1 + c + 1])
                    else:
                        last_ = nc.scalar.activation(hT[:, q % 2, :, :].rearrange("p c t -> p (c t)"),
                                                     ps[:, bank:bank + 2, :].rearrange("p b t -> p (b t)"),
                                                     ACT.Gelu_apprx_tanh)
                    last_.then_inc(s.gelu_done, 1)
                    if not last or q + 1 < s.body:
                        evacuate(t + 1, q + 1)

            evacuate(0, 0)
            bodies(engine_loop(act), s.tiles // s.body, body)
            if zero:
                for j in range(NB):
                    act.wait_ge(s.z_ready, j + 1)
                    nc.scalar.activation(z_squares(j), z[:, j * TPB:(j + 1) * TPB, :], ACT.Square).then_inc(s.z_sq, 1)
                act.wait_ge(s.std_in, 2)
                nc.scalar.activation(t32[:], var[:], ACT.Sqrt).then_inc(s.std_ready, 1)

        def act_attention(act, s):
            act_norm(act, s)

            def compressed(j):
                for w, dst in ((0, cq[:, j % 2, :]), (1, ckv[:, j * BLK:(j + 1) * BLK])):
                    act.wait_ge(s.c_done, 2 * j + w + 1)
                    if w == 0 and j >= 2:
                        act.wait_ge(s.qkv_done, j - 1)
                    nc.scalar.copy(dst, ps[0:32, 4 + w, :]).then_inc(s.c_evac, 1)

            if s.kind == "attn1":
                compressed(0)
            for j in range(NB):
                if s.kind == "attn1" and j + 1 < NB:
                    compressed(j + 1)
                for w in range(2):
                    for a in range(2):
                        act.wait_ge(s.r_ready, 4 * j + 2 * w + a + 1)
                        if a == 0 and j >= 1:
                            act.wait_ge(s.parts_out[w], 16 * PARTS * j)
                        nc.scalar.copy(parts[:, w, a, :], qk_f[:, 2 + 2 * w + a, :]).then_inc(s.p_copied, 1)

            def exps(i, r):
                n = i * EXP_ROUND + r
                for g, (hf, kt) in enumerate(s.groups):
                    slot = (s.G * r + g) % W_RING
                    act.wait_ge(s.st_done, n * s.G + g + 1)
                    act.wait_ge(s.pv_done, PV0 + n * s.G + g - 3)
                    for m, lo, w in spans(s, hf, kt):
                        st = ps[:, 2 * (g % 2) + m:2 * (g % 2) + m + w, lo:BLK]
                        nc.scalar.activation(span_of(ws[:, slot, :], m, lo, w), st, ACT.Exp,
                                             scale=s.scale)
                        last = nc.scalar.activation(span_of(wp[:, 0, slot, :], m, lo, w), st, ACT.Exp,
                                                    scale=s.scale)
                    last.then_inc(s.exp_done, 1)

            act.sem_inc(s.exp_done, 2)
            with act.Fori(0, HEADS // EXP_ROUND) as i:
                for r in range(EXP_ROUND):
                    exps(i, r)
            for j in range(NB):
                act.wait_ge(s.at_done, j + 1)
                nc.scalar.copy(xnT[:, j * BLK:(j + 1) * BLK], ps[:, j % 2, :]).then_inc(s.at_evac, 1)

        @block.scalar
        def _(act):
            for s in S:
                (act_ffn if s.kind.startswith("ffn") else act_attention)(act, s)

        def pe_transposes(pe, s, then):
            for g in range(NB):
                pe.wait_ge(s.xn_ready, NB * s.k + g + 1)
                if g >= 2:
                    pe.wait_ge(s.tr_evac, NB * s.k + g - 1)
                for t in range(TPB):
                    mm = nc.tensor.transpose(ps[:, g % 2, t * P:(t + 1) * P], xn[:, g * TPB + t, :], ident)
                mm.then_inc(s.tr_done, 1)
                if g >= 1:
                    then(g - 1)
            then(NB - 1)

        def pe_ffn(pe, s):
            L = int(s.kind[3])

            def logits(g):
                pe.wait_ge(s.tr_evac, NB * s.k + g + 1)
                for t in range(g * TPB, (g + 1) * TPB):
                    mm = nc.tensor.matmul(ps[:, 6, t * E:(t + 1) * E], xnT[:, t * P:(t + 1) * P], rw[L][:],
                                          start=True, stop=True)
                mm.then_inc(s.lg_done, 1)

            pe_transposes(pe, s, logits)
            pe.wait_ge(s.sel_ready, s.ffns + 1)
            sel = sel_bf[:].rearrange("p t e -> p (t e)")
            nc.tensor.matmul(ps[:, 6, 0:NT * E], tri_bf, sel, start=True, stop=True)
            nc.tensor.matmul(ps[:, 7, 0:NT * E], ones_bf[:], sel, start=True, stop=True).then_inc(s.cnt_done, 1)
            for h in range(HOT_CHUNKS):
                pe.wait_ge(s.hot_ready, HOT_CHUNKS * s.ffns + h + 1)
                for g in range(h * 2 * NT // HOT_CHUNKS, (h + 1) * 2 * NT // HOT_CHUNKS):
                    mm = nc.tensor.matmul(ps[:, 5, 0:2 * HALVES], hot_place[:, g, :],
                                          hot_half[:, g, :, :].rearrange("p a c -> p (a c)"), start=(g == 0),
                                          stop=(g == 2 * NT - 1))
            mm.then_inc(s.tab_done, 1)
            pe.wait_ge(s.idx_ready, s.ffns + 1)

            def turn(i, q, first):
                t, r = i * s.body + q, q % X_RING
                pe.wait_ge(xs_in[r], 32 * (s.ring0 + 1 + i * (s.body // X_RING) + q // X_RING))
                if not first or q >= 2:
                    pe.wait_ge(s.xt_evac, t - 1)
                for h in range(2):
                    mm = nc.tensor.transpose(ps[:, q % 2, h * P:(h + 1) * P], xs[:, r, h, :], ident)
                mm.then_inc(s.tp_done, 1)

            def up(i, q, first):
                t, n, w = i * s.body + q, q // s.share, q // s.share % s.w_slots
                pe.wait_ge(s.xt_evac, t + 1)
                loads = s.body // s.share // s.w_slots
                pe.wait_ge(w_in[w], 16 * (s.w0[w] + 1 + i * loads + n // s.w_slots))
                if not first or q >= 2:
                    pe.wait_ge(s.gelu_done, t - 1)
                for c in range(NC):
                    mm = nc.tensor.matmul(ps[:, 2 + 2 * (q % 2) + c // 2, c % 2 * TS:(c % 2 + 1) * TS],
                                          wts[:, w, c * P:(c + 1) * P], xt[:, q % 2, :], start=True, stop=True)
                mm.then_inc(s.up_done, 1)

            def down(i, q, first):
                t, w = i * s.body + q, q // s.share % s.w_slots
                pe.wait_ge(s.gelu_done, t + 1)
                if not first or q >= 2:
                    pe.wait_ge(s.y_ready, t - 1)
                for h in range(2):
                    for c in range(NC):
                        mm = nc.tensor.matmul(ps[:, 6 + q % 2, h * D:(h + 1) * D], hT[:, q % 2, c, h * P:(h + 1) * P],
                                              wts[:, w, O_W2 + c * D:O_W2 + (c + 1) * D], start=(c == 0),
                                              stop=(c == NC - 1))
                mm.then_inc(s.down_done, 1)

            def body(i, first, last):
                for q in range(s.body):
                    up(i, q, first)
                    if q + 1 < s.body:
                        turn(i, q + 1, first)
                    elif not last:
                        turn(i + 1, 0, False)
                    if q:
                        down(i, q - 1, first)
                    elif not first:
                        down(i - 1, s.body - 1, False)
                if last:
                    down(i, s.body - 1, False)

            turn(0, 0, True)
            bodies(engine_loop(pe), s.tiles // s.body, body)

        def pe_attention(pe, s):
            pe_transposes(pe, s, lambda g: None)
            xb = lambda j: xnT[:, j * BLK:(j + 1) * BLK]
            pe.wait_ge(s.tr_evac, NB * (s.k + 1))
            if s.kind == "attn0":
                for j in range(NB):
                    if j >= 2:
                        pe.wait_ge(s.qkv_free, 2 * (j - 1))
                    for w in range(4):
                        mm = nc.tensor.matmul(ps[:, qkv_bank(s, j, w), :], wqkv[:, w, :], xb(j), start=True, stop=True)
                    mm.then_inc(s.qkv_done, 1)
            else:
                def compress(j):
                    if j >= 1:
                        pe.wait_ge(s.c_evac, 2 * j)
                    for w in range(2):
                        nc.tensor.matmul(ps[0:32, 4 + w, :], wd[:, w, :], xb(j), start=True,
                                         stop=True).then_inc(s.c_done, 1)

                compress(0)
                for j in range(NB):
                    if j + 1 < NB:
                        compress(j + 1)
                    pe.wait_ge(s.c_evac, 2 * j + 2)
                    if j >= 2:
                        pe.wait_ge(s.qkv_free, 2 * (j - 1))
                    nc.tensor.matmul(ps[:, qkv_bank(s, j, 0), :], wu[:, 0, :], cq[:, j % 2, :], start=True, stop=True)
                    nc.tensor.matmul(ps[:, qkv_bank(s, j, 2), :], wu[:, 1, :], ckv[:, j * BLK:(j + 1) * BLK],
                                     start=True, stop=True).then_inc(s.qkv_done, 1)
            pe.wait_ge(s.qkv_free, 2 * (NB - 1))
            for j in range(NB):
                if j >= 2:
                    pe.wait_ge(s.v_evac, 2 * j - 2)
                for t in range(TPB):
                    c = (j * TPB + t) * P
                    lhs, rhs = (xnT[:, c:c + P], wqkv[:, 4, :]) if s.kind == "attn0" else (ckv[:, c:c + P], wu[:, 2, :])
                    mm = nc.tensor.matmul(ps[:, 6 + j % 2, t * P:(t + 1) * P], lhs, rhs, start=True, stop=True)
                mm.then_inc(s.v_done, 1)
            pe.wait_ge(s.v_evac, 2 * NB)
            pe.wait_ge(s.qkv_free, 2 * NB)

            def head_max(i, r, m, q, c, w):
                n = i * RING + r
                if m == 0:
                    pe.wait_ge(s.qk_in[r], 16 * LOADS * (i + 1))
                pe.wait_ge(s.red_done, n * s.M + m + 1)
                diag = s.causal and c + w == (q + 1) * P
                mm = nc.tensor.matmul(ps[:, 4 + m % 2, 0:w], qs[0:KM, r, q * P:(q + 1) * P],
                                      ks[0:KM, r, c:c + w], start=True, stop=not diag, skip_group_check=True)
                if diag:
                    mm = nc.tensor.matmul(ps[:, 4 + m % 2, w - P:w], ident_bf, maskS, start=False, stop=True,
                                          skip_group_check=True)
                mm.then_inc(s.sm_done, 1)

            def turn_max(i, r):
                n = i * RING + r
                pe.wait_ge(s.row_done, n + 1)
                pe.wait_ge(s.mf_ready, n + 1)
                nc.tensor.transpose(ps[0:NKT, 6 + r % 2, TURNED:TURNED + P], rowmax[:, r, 0, :],
                                    ident).then_inc(s.mt_done, 1)

            def scores(i, r, g):
                n, (hf, kt) = i * RING + r, s.groups[g]
                if g == 0:
                    pe.wait_ge(s.m_in[r], 16 * PARTS * (i + 1))
                pe.wait_ge(s.exp_done, n * s.G + g + 1)
                for m in range(2):
                    off = kt + m - 4 * hf
                    diag = s.causal and off >= 0
                    lo = off * P if diag else 0
                    mm = nc.tensor.matmul(ps[:, 2 * (g % 2) + m, lo:BLK], ks[:, r, (kt + m) * P:(kt + m + 1) * P],
                                          qs[:, r, hf * BLK + lo:(hf + 1) * BLK], start=True, stop=not diag,
                                          skip_group_check=True)
                    if diag:
                        mm = nc.tensor.matmul(ps[:, 2 * (g % 2) + m, lo:lo + P], ident_bf, maskT, start=False,
                                              stop=True, skip_group_check=True)
                mm.then_inc(s.st_done, 1)

            def values(i, r, g):
                n, (hf, kt) = i * RING + r, s.groups[g]
                slot = (s.G * r + g) % W_RING
                pe.wait_ge(s.exp_done, n * s.G + g + 1 + 2)
                own, done = (s.on_dve, s.sub_dve) if g in s.on_dve else (s.on_pool, s.sub_pool)
                pe.wait_ge(done, n * len(own) + own.index(g) + 1)
                if g == 0:
                    pe.wait_ge(s.nrm_done, n + 1)
                for m in range(2):
                    off = kt + m - 4 * hf
                    for qt in range(max(0, off) if s.causal else 0, TPB):
                        end = kt + m == (4 * hf + qt if s.causal else NKT - 1)
                        for a in range(2):
                            q = hf * TPB + qt
                            mm = nc.tensor.matmul(ps[:, 6 + r % 2, q * VW:(q + 1) * VW],
                                                  wp[:, a, slot, m * BLK + qt * P:m * BLK + (qt + 1) * P],
                                                  vr[:, r, kt + m, :], start=(g == 0 and m == 0 and qt == 0 and a == 0),
                                                  stop=(end and a == 1), skip_group_check=True)
                mm.then_inc(s.pv_done, 1)

            def step(i, r, ahead):
                one, two = (i + (r + 1) // RING, (r + 1) % RING), (i + (r + 2) // RING, (r + 2) % RING)
                before = (i - 1, RING - 1) if r == 0 else (i, r - 1)
                for g in range(s.G):
                    scores(i, r, g)
                    if g >= LAG:
                        values(i, r, g - LAG)
                    elif type(i) is not int or i or r:
                        values(*before, s.G + g - LAG)
                    if g == LAG - 1 and ahead >= 1:
                        turn_max(*one)
                    if ahead >= 2:
                        for piece in s.pieces[g]:
                            head_max(*two, *piece)

            pe.sem_inc(s.pv_done, PV0)
            for piece in s.all_pieces:
                head_max(0, 0, *piece)
            turn_max(0, 0)
            for piece in s.all_pieces:
                head_max(0, 1, *piece)

            def loop(count):
                with pe.Fori(0, count) as i:
                    yield i

            rounds(loop, step)
            for g in range(s.G - LAG, s.G):
                values(HEADS // RING - 1, RING - 1, g)
            L = int(s.kind[4])
            def project(j):
                pe.wait_ge(s.at_evac, j + 1)
                if j >= 2:
                    pe.wait_ge(s.wo_free, j - 1)
                for t in range(TPB):
                    c = (j * TPB + t) * P
                    mm = nc.tensor.matmul(ps[:, 2 + j % 2, t * P:(t + 1) * P], xnT[:, c:c + P],
                                          wo[L][:], start=True, stop=True)
                mm.then_inc(s.wo_done, 1)

            pe.wait_ge(s.nrm_done, HEADS + 2)
            for j in range(NB):
                if j >= 2:
                    pe.wait_ge(s.at_evac, j - 1)
                for t in range(TPB):
                    mm = nc.tensor.transpose(ps[:, j % 2, t * P:(t + 1) * P], xn[:, j * TPB + t, :], ident)
                mm.then_inc(s.at_done, 1)
                if j >= 1:
                    project(j - 1)
            project(NB - 1)

        @block.tensor
        def _(pe):
            pe.wait_ge(c_ready, 1)
            for s in S:
                (pe_ffn if s.kind.startswith("ffn") else pe_attention)(pe, s)

        def pool_ffn(pool, s):
            def pick(t):
                for h in range(2):
                    nc.gpsimd.indirect_dma_start(
                        out=xs[:, t % X_RING, h, :], out_offset=None, in_=xd[:],
                        in_offset=bass.IndirectOffsetOnAxis(ap=token_of[:, 2 * t + h:2 * t + h + 1], axis=0),
                    ).then_inc(xs_in[t % X_RING], 16)

            def put(t):
                pool.wait_ge(s.y_ready, t + 1)
                for h in range(2):
                    nc.gpsimd.indirect_dma_start(
                        out=yd[:], out_offset=bass.IndirectOffsetOnAxis(ap=row_of[:, 2 * t + h:2 * t + h + 1], axis=0),
                        in_=ys[:, t % X_RING, h, :], in_offset=None).then_inc(y_out[t % X_RING], 16)

            pool.wait_ge(xd_out, 16 * (s.ffns + 1))
            pool.wait_ge(s.idx_ready, s.ffns + 1)
            for t in range(X_RING):
                pick(t)
            for t in range(s.tiles):
                if t + X_RING < s.tiles:
                    pool.wait_ge(s.tp_done, t + 1)
                    pick(t + X_RING)
                if t:
                    put(t - 1)
            put(s.tiles - 1)

        def pool_attention(pool, s):
            v = nc.gpsimd
            st = Steps(pool, s.pool_step)
            link = st.link

            def split_max(i, r):
                pool.wait_ge(s.mf_ready, i * RING + r + 3)
                link(v.tensor_tensor(mp[:, r, 0, :], mf[:, r % 2, :], nil[:], ALU.add))
                link(v.tensor_tensor(mrest[:], mf[:, r % 2, :], mp[:, r, 0, :], ALU.subtract))
                link(v.tensor_tensor(mp[:, r, 1, :], mrest[:], nil[:], ALU.add))
                v.tensor_tensor(mp[:, r, 2, :], mrest[:], mp[:, r, 1, :], ALU.subtract).then_inc(s.msplit, 1)

            def step(i, r, ahead):
                for g in range(s.G):
                    if g == s.split_at and ahead >= 1:
                        split_max(i + (r + 1) // RING, (r + 1) % RING)
                    if g in s.on_pool:
                        pool.wait_ge(s.exp_done, (i * RING + r) * s.G + g + 3)
                        subtract(v, s, r, g, s.sub_pool)

            pool.sem_inc(s.msplit, 2)
            split_max(0, 0)
            rounds(lambda count: st.loop(count, 3 * RING), step)

        @block.gpsimd
        def _(pool):
            for s in S:
                if s.kind.startswith("ffn"):
                    pool_ffn(pool, s)
                else:
                    pool_attention(pool, s)

        @block.vector
        def _(dve):
            st = Steps(dve, dve_step)
            link = st.link
            v = nc.vector
            dve.wait_ge(par_in, 16 * N_SMALL)
            link(v.memset(ones_bf[:], 1.0))
            link(v.memset(nil[:], 0.0))
            link(v.tensor_scalar(lane_t[:], spare_row[:, 0:1], float(2 * T), None, ALU.subtract))
            link(v.memset(vall[:, :, :, VW - 1:VW], 1.0))
            link(v.memset(ks[64:P, :, :], -1.0))
            link(v.memset(qs[64:P, :, :], 0.0))
            link(v.tensor_copy(cbf[:], consts[:, 0:4 * P]))
            dve.sem_inc(c_ready, 1)
            dve.wait_ge(x_in, 16)

            def normalise():
                for g in range(4):
                    t = slice(g * 8, (g + 1) * 8)
                    link(v.tensor_reduce(mean[:, t], x[:, t, :], AX.X, ALU.add))
                    link(v.tensor_scalar(mean[:, t], mean[:, t], 1.0 / D, None, ALU.mult))
                    v.tensor_tensor(xn[:, t, :], x[:, t, :], bcast(mean[:, t], 2, D),
                                    ALU.subtract).then_inc(s.xc_ready, 1)
                for g in range(4):
                    dve.wait_ge(s.sq_ready, 4 * s.k + g + 1)
                    link(v.tensor_reduce(var[:, g * 8:(g + 1) * 8],
                                         xnT[:, g * 1024:(g + 1) * 1024].rearrange("p (t d) -> p t d", d=D),
                                         AX.X, ALU.add))
                v.tensor_scalar(var[:], var[:], 1.0 / D, 1e-5, ALU.mult, ALU.add).then_inc(s.std_in, 1)
                dve.wait_ge(s.std_ready, 1)
                inverse_root()
                for g in range(NB):
                    t = slice(g * TPB, (g + 1) * TPB)
                    v.tensor_tensor(xn[:, t, :], xn[:, t, :], bcast(rstd[:, t], 2, D),
                                    ALU.mult).then_inc(s.xn_ready, 1)

            def inverse_root(t=slice(0, NT)):
                link(v.reciprocal(rstd[:, t], t32[:, t]))
                link(v.tensor_tensor(t32[:, t], rstd[:, t], rstd[:, t], ALU.mult))
                link(v.tensor_tensor(t32[:, t], t32[:, t], var[:, t], ALU.mult))
                link(v.tensor_scalar(t32[:, t], t32[:, t], -0.5, 1.5, ALU.mult, ALU.add))
                link(v.tensor_tensor(rstd[:, t], rstd[:, t], t32[:, t], ALU.mult))

            def first_of(dst, value, top):
                link(v.tensor_tensor(r2[:], value, bcast(top[:], 2, E), ALU.is_equal))
                link(v.tensor_tensor(r2[:], r2[:], bcast(first_pref, 1, NT), ALU.mult))
                link(v.tensor_reduce(pw1[:], r2[:], AX.X, ALU.max))
                link(v.tensor_tensor(dst, r2[:], bcast(pw1[:], 2, E), ALU.is_equal))

            def top_two(value):
                link(v.tensor_reduce(top1[:], value, AX.X, ALU.max))
                first_of(sel1[:], value, top1)
                link(v.scalar_tensor_tensor(value, sel1[:], -3e38, value, ALU.mult, ALU.add))
                link(v.tensor_reduce(top2[:], value, AX.X, ALU.max))
                first_of(sel2[:], value, top2)

            def route(s):
                dve.wait_ge(s.lg_done, NB * (s.ffns + 1))
                logits = ps[:, 6, 0:NT * E].rearrange("p (t e) -> p t e", e=E)
                if s.L == 0:
                    link(v.tensor_tensor(lg[:], logits, bcast(rb[:], 1, NT), ALU.add))
                    top_two(lg[:])
                    v.tensor_tensor(top2[:], top2[:], top1[:], ALU.subtract).then_inc(s.ex_in, 1)
                else:
                    link(v.tensor_copy(lg[:], logits))
                    link(v.tensor_reduce(top1[:], lg[:], AX.X, ALU.max))
                    v.tensor_tensor(r1[:], lg[:], bcast(top1[:], 2, E), ALU.subtract).then_inc(s.ex_in, 1)
                    dve.wait_ge(s.ex_ready, s.ffns + 1)
                    link(v.tensor_reduce(t32[:], r1[:], AX.X, ALU.add))
                    link(v.reciprocal(t32[:], t32[:]))
                    link(v.tensor_tensor(r1[:], r1[:], bcast(t32[:], 2, E), ALU.mult))
                    top_two(r1[:])
                    link(v.tensor_copy(pw1[:], top1[:]))
                    link(v.tensor_copy(pw2[:], top2[:]))
                v.tensor_tensor(sel_bf[:], sel1[:], sel2[:], ALU.add).then_inc(s.sel_ready, 1)
                if s.L == 0:
                    dve.wait_ge(s.ex_ready, s.ffns + 1)
                    link(v.tensor_scalar(pw1[:], t32[:], 1.0, None, ALU.add))
                    link(v.reciprocal(pw1[:], pw1[:]))
                    link(v.tensor_tensor(pw2[:], pw1[:], t32[:], ALU.mult))
                dve.wait_ge(s.cnt_done, s.ffns + 1)
                tot = ps[:, 7, 0:NT * E].rearrange("p (t e) -> p t e", e=E)
                a, b = r1, r2
                link(v.memset(a[:, 0:1, :], 0.0))
                link(v.tensor_copy(a[:, 1:NT, :], tot[:, 0:NT - 1, :]))
                k = 1
                while k < NT:
                    link(v.tensor_copy(b[:, 0:k, :], a[:, 0:k, :]))
                    link(v.tensor_tensor(b[:, k:NT, :], a[:, k:NT, :], a[:, 0:NT - k, :], ALU.add))
                    a, b = b, a
                    k *= 2
                link(v.tensor_tensor(lg[:], ps[:, 6, 0:NT * E].rearrange("p (t e) -> p t e", e=E), a[:], ALU.add))
                if s.L == 0:
                    link(v.tensor_tensor(total[:], a[:, NT - 1, :], tot[:, NT - 1, :], ALU.add))
                    link(v.tensor_tensor(fit[:], bcast(total[:], 2, T // TS), bcast(tile_start[:, 0:T // TS], 1, E),
                                         ALU.is_gt))
                    link(v.tensor_reduce(n_tiles[:], fit[:], AX.X, ALU.add))
                    c, d = ends, ends2
                    link(v.tensor_copy(c[:], n_tiles[:]))
                    k = 1
                    while k < E:
                        link(v.tensor_copy(d[:, 0:k], c[:, 0:k]))
                        link(v.tensor_tensor(d[:, k:E], c[:, k:E], c[:, 0:E - k], ALU.add))
                        c, d = d, c
                        k *= 2
                    link(v.tensor_tensor(base[:], c[:], n_tiles[:], ALU.subtract))
                    link(v.tensor_scalar(base[:], base[:], float(TS), None, ALU.mult))
                    link(v.tensor_scalar(c[:], c[:], float(TS), None, ALU.mult))
                    link(v.tensor_tensor(tile_cmp[:], bcast(c[0:1, :], 1, TILES[0]), bcast(tile_start[0:1, :], 2, E),
                                         ALU.is_le))
                    link(v.tensor_reduce(tile_f[:], tile_cmp[:], AX.X, ALU.add))
                    link(v.tensor_scalar(tile_f[:], tile_f[:], float(E - 1), None, ALU.min))
                    v.tensor_copy(tile_expert[:], tile_f[:]).then_inc(s.map_ready, 1)
                    first_slot = base[:]
                else:
                    link(v.tensor_scalar(b[:], lg[:], float(CAPACITY), None, ALU.is_lt))
                    for k, (sel, pw) in enumerate(((sel1, pw1), (sel2, pw2))):
                        link(v.tensor_tensor(a[:], sel[:], b[:], ALU.mult))
                        link(v.tensor_reduce(room[:, k, :], a[:], AX.X, ALU.add))
                        link(v.tensor_tensor(pw[:], pw[:], room[:, k, :], ALU.mult))
                    link(v.tensor_scalar(lg[:], lg[:], float(CAPACITY - 1), None, ALU.min))
                    first_slot = expert_base
                    dve.sem_inc(s.map_ready, 1)
                link(v.tensor_tensor(lg[:], lg[:], bcast(first_slot, 1, NT), ALU.add))
                for k, sel in enumerate((sel1, sel2)):
                    link(v.tensor_tensor(a[:], sel[:], lg[:], ALU.mult))
                    link(v.tensor_reduce(slot_f[:, k, :], a[:], AX.X, ALU.add))
                slots = slot_f[:].rearrange("p k t -> p (k t)")
                if s.L == 1:
                    link(v.tensor_scalar(room[:], room[:], -NO_ROOM, NO_ROOM, ALU.mult, ALU.add))
                    link(v.tensor_tensor(slot_f[:], slot_f[:], room[:], ALU.add))
                link(v.tensor_copy(slot_i[:], slots))
                link(v.tensor_scalar(slot_i[:], slot_i[:], P - 1, None, ALU.bitwise_and))
                link(v.tensor_copy(place[:], slot_i[:]))
                link(v.tensor_tensor(half[:], slots, place[:], ALU.subtract))
                for h in range(HOT_CHUNKS):
                    n = 2 * NT // HOT_CHUNKS
                    g = slice(h * n, (h + 1) * n)
                    link(v.tensor_tensor(hot_one[:, g, :], bcast(half_start, 1, n), bcast(half[:, g], 2, HALVES),
                                         ALU.is_equal))
                    link(v.tensor_tensor(hot_half[:, g, 0, :], hot_one[:, g, :], bcast(group_no[:, g], 2, HALVES),
                                         ALU.mult))
                    link(v.tensor_scalar(hot_half[:, g, 1, :], hot_one[:, g, :], lane, None, ALU.mult))
                    v.tensor_tensor(hot_place[:, g, :], bcast(count_up, 1, n), bcast(place[:, g], 2, P),
                                    ALU.is_equal).then_inc(s.hot_ready, 1)
                dve.wait_ge(s.tab_done, s.ffns + 1)
                group, part = ps[:, 5, 0:HALVES], ps[:, 5, HALVES:2 * HALVES]
                link(v.tensor_scalar(used[:], group, 0.0, None, ALU.is_gt))
                link(v.tensor_scalar(late[:], group, float(NT), None, ALU.is_gt))
                link(v.tensor_scalar(row_f[:], group, float(P), float(-P), ALU.mult, ALU.add))
                link(v.tensor_tensor(row_f[:], row_f[:], part, ALU.add))
                link(v.scalar_tensor_tensor(tok_f[:], late[:], float(-T), row_f[:], ALU.mult, ALU.add))
                link(v.tensor_scalar(tok_f[:], tok_f[:], 0.0, None, ALU.max))
                link(v.tensor_copy(token_of[:], tok_f[:]))
                link(v.tensor_tensor(row_f[:], row_f[:], spare_row, ALU.subtract))
                link(v.tensor_tensor(row_f[:], row_f[:], used[:], ALU.mult))
                link(v.tensor_tensor(row_f[:], row_f[:], spare_row, ALU.add))
                v.tensor_copy(row_of[:], row_f[:]).then_inc(s.idx_ready, 1)

            def ffn(s):
                normalise()
                route(s)
                link(v.scalar_tensor_tensor(x[:], bcast((lnb if s.L == 0 else ffn_bias)[:], 1, NT), 0.5, x[:],
                                            ALU.mult, ALU.add))
                if s.L == 1:
                    link(v.tensor_scalar(pw1[:], pw1[:], 0.5, None, ALU.mult))
                    link(v.tensor_scalar(pw2[:], pw2[:], 0.5, None, ALU.mult))

                def body(i, first, last):
                    for q in range(s.body):
                        t, r = i * s.body + q, q % X_RING
                        dve.wait_ge(s.down_done, t + 1)
                        if not first or q >= X_RING:
                            dve.wait_ge(y_out[r], 32 * (s.ring0 + i * (s.body // X_RING) + q // X_RING))
                        src = ps[:, 6 + q % 2, 0:2 * D].rearrange("p (h d) -> p h d", h=2)
                        if s.L == 0:
                            w = q // s.share % s.w_slots
                            ins_ = v.tensor_tensor(ys[:, r, :, :], src, bcast(wts[:, w, O_B2:O_B2 + D], 1, 2), ALU.add)
                        else:
                            ins_ = v.tensor_copy(ys[:, r, :, :], src)
                        ins_.then_inc(s.y_ready, 1)

                bodies(engine_loop(dve), s.tiles // s.body, body)
                for j in range(NB):
                    t = slice(j * TPB, (j + 1) * TPB)
                    dve.wait_ge(gathered[j], 16 * 2 * (s.ffns + 1))
                    own = range(TPB)
                    if s.L == 1:
                        for k, pw in enumerate((pw1, pw2)):
                            for q in own:
                                c = j * TPB + q
                                ins_ = v.scalar_tensor_tensor(x[:, c, :], both[:, c, k, :], pw[:, c:c + 1], x[:, c, :],
                                                              ALU.mult, ALU.add)
                            link(ins_)
                        continue
                    for q in own:
                        c = j * TPB + q
                        ins_ = v.scalar_tensor_tensor(z[:, c, :], both[:, c, 0, :], pw1[:, c:c + 1], xn[:, c, :],
                                                      ALU.mult, ALU.add)
                    link(ins_)
                    for q in own:
                        c = j * TPB + q
                        ins_ = v.scalar_tensor_tensor(z[:, c, :], both[:, c, 1, :], pw2[:, c:c + 1], z[:, c, :],
                                                      ALU.mult, ALU.add)
                    link(ins_)
                    link(v.tensor_reduce(stat[:], z[:, t, :], AX.X, ALU.add))
                    link(v.tensor_scalar(stat[:], stat[:], 1.0 / D, None, ALU.mult))
                    v.tensor_tensor(z[:, t, :], z[:, t, :], bcast(stat[:], 2, D), ALU.subtract).then_inc(s.z_ready, 1)
                    if j:
                        sum_squares(s, j - 1)
                if s.L == 0:
                    dve.wait_ge(s.z_ready, NB)
                    sum_squares(s, NB - 1)
                    v.tensor_scalar(var[:], var[:], 1.0 / D, 1e-12, ALU.mult, ALU.add).then_inc(s.std_in, 1)
                    dve.wait_ge(s.std_ready, 2)
                    inverse_root()
                    for j in range(NB):
                        t = slice(j * TPB, (j + 1) * TPB)
                        for q in range(TPB):
                            c = j * TPB + q
                            ins_ = v.scalar_tensor_tensor(z[:, c, :], z[:, c, :], rstd[:, c:c + 1], lnw[:],
                                                          ALU.mult, ALU.mult)
                        link(ins_)
                        link(v.scalar_tensor_tensor(x[:, t, :], z[:, t, :], 0.5, x[:, t, :], ALU.mult, ALU.add))

            def sum_squares(s, j):
                dve.wait_ge(s.z_sq, j + 1)
                link(v.tensor_reduce(var[:, j * TPB:(j + 1) * TPB], z_squares(j), AX.X, ALU.add))

            def first_rest(s, m):
                w = m % 2
                dve.wait_ge(s.p_copied, 2 * m + 1)
                v.tensor_tensor(qk_f[:, 3 + 2 * w, :], qk_f[:, 2 + 2 * w, :], parts[:, w, 0, :],
                                ALU.subtract).then_inc(s.r_ready, 1)

            def third_part(s, m):
                w = m % 2
                dve.wait_ge(s.r_ready, 2 * m + 2)
                dve.wait_ge(s.p_copied, 2 * m + 2)
                v.tensor_tensor(parts[:, w, 2, :], qk_f[:, 3 + 2 * w, :], parts[:, w, 1, :],
                                ALU.subtract).then_inc(s.parts_ready, 1)

            def attention(s):
                normalise()
                rope = s.kind == "attn0"
                for j in range(NB):
                    pos = slice((j % 2) * BLK, (j % 2) * BLK + BLK)
                    for w in range(2):
                        dve.wait_ge(s.qkv_done, j + 1)
                        if j >= 1:
                            dve.wait_ge(s.parts_ready, 2 * (j - 1) + w + 1)
                        if rope:
                            link(v.scalar_tensor_tensor(qk_f[:, 0, :], ps[:, qkv_bank(s, j, 2 * w), :], bqk[:, 2 * w:2 * w + 1],
                                                        trig[:, 0, pos], ALU.add, ALU.mult))
                            ins_ = v.scalar_tensor_tensor(qk_f[:, 1, :], ps[:, qkv_bank(s, j, 2 * w + 1), :],
                                                          bqk[:, 2 * w + 1:2 * w + 2], trig[:, 1, pos],
                                                          ALU.add, ALU.mult)
                            ins_.then_inc(s.qkv_free, 1)
                            dve.wait_ge(s.qkv_free, 2 * j + w + 1)
                            v.tensor_tensor(qk_f[:, 2 + 2 * w, :], qk_f[:, 0, :], qk_f[:, 1, :],
                                            ALU.add).then_inc(s.r_ready, 1)
                        else:
                            link(v.tensor_copy(qk_f[:, 2 + 2 * w, :], ps[:, qkv_bank(s, j, 2 * w), :]))
                            dve.sem_inc(s.qkv_free, 1)
                            dve.sem_inc(s.r_ready, 1)
                        m = 2 * j + w
                        if m:
                            third_part(s, m - 1)
                        dve.wait_ge(s.r_ready, 2 * m + 1)
                        first_rest(s, m)
                third_part(s, 2 * NB - 1)
                for j in range(NB):
                    b, k0 = j // 2, (j % 2) * TPB
                    dst = [vall[:, b * H:(b + 1) * H, k0:k0 + TPB, a * DH:(a + 1) * DH].rearrange("p h k d -> p k h d")
                           for a in range(PARTS)]

                    def heads(ap):
                        return ap.rearrange("p (k h d) -> p k h d", k=TPB, h=H)

                    vf, rest = heads(qk_f[:, 0, :]), heads(qk_f[:, 1, :])
                    dve.wait_ge(s.v_done, j + 1)
                    if rope:
                        ins_ = v.tensor_tensor(qk_f[:, 0, :].rearrange("p (k c) -> p k c", k=TPB),
                                               ps[:, 6 + j % 2, :].rearrange("p (k c) -> p k c", k=TPB),
                                               bcast(bv[:], 1, TPB), ALU.add)
                    else:
                        ins_ = v.tensor_copy(qk_f[:, 0, :], ps[:, 6 + j % 2, :])
                    ins_.then_inc(s.v_evac, 1)
                    dve.wait_ge(s.v_evac, 2 * j + 1)
                    link(v.tensor_copy(dst[0], vf))
                    link(v.tensor_tensor(rest, vf, dst[0], ALU.subtract))
                    link(v.tensor_copy(dst[1], rest))
                    v.tensor_tensor(dst[2], rest, dst[1], ALU.subtract).then_inc(s.v_evac, 1)
                    dve.wait_ge(s.v_evac, 2 * j + 2)

                def reduce(i, r, m, q, c, w):
                    n = i * RING + r
                    dve.wait_ge(s.sm_done, n * s.M + m + 1)
                    v.tensor_reduce(rowmax[:, r, c // BLK, q:q + 1], ps[:, 4 + m % 2, 0:w], AX.X,
                                    ALU.max).then_inc(s.red_done, 1)
                    if m == s.M - 1:
                        q0 = NKT // 2 if s.causal else 0
                        dve.wait_ge(s.red_done, (n + 1) * s.M + 2)
                        v.tensor_tensor(rowmax[:, r, 0, q0:], rowmax[:, r, 0, q0:], rowmax[:, r, 1, q0:],
                                        ALU.max).then_inc(s.row_done, 1)

                def fetch_max(i, r):
                    n = i * RING + r
                    dve.wait_ge(s.mt_done, n + 1)
                    dve.wait_ge(s.msplit, n + 1)
                    v.tensor_scalar(mf[:, r % 2, :], ps[0:NKT, 6 + r % 2, TURNED:TURNED + P], -SHIFT / s.scale, None,
                                    ALU.add).then_inc(s.mf_ready, 1)

                def sub(i, r, g):
                    dve.wait_ge(s.exp_done, (i * RING + r) * s.G + g + 3)
                    subtract(v, s, r, g, s.sub_dve)

                def divide(i, r):
                    n = i * RING + r
                    o = ps[:, 6 + r % 2, 0:NKT * VW].rearrange("p (q c) -> p q c", c=VW)
                    tiles = bass.ds((i // (H // RING)) * NKT, NKT)
                    head = bass.ds((i % (H // RING)) * RING * DH + r * DH, DH)
                    dve.wait_ge(s.pv_done, PV0 + (n + 1) * s.G)
                    dve.wait_ge(s.nrm_done, n + 2)
                    link(v.reciprocal(rec[:], o[:, :, VW - 1]))
                    link(v.tensor_reduce(osum[:], o[:, :, 0:PARTS * DH].rearrange("p q (a d) -> p q d a", a=PARTS),
                                         AX.X, ALU.add))
                    v.tensor_tensor(xn[:, tiles, head], osum[:], bcast(rec[:], 2, DH), ALU.mult).then_inc(s.nrm_done, 1)

                def step(i, r, ahead):
                    one, two = (i + (r + 1) // RING, (r + 1) % RING), (i + (r + 2) // RING, (r + 2) % RING)
                    before = (i - 1, RING - 1) if r == 0 else (i, r - 1)
                    for g in range(s.G):
                        if ahead >= 2:
                            for piece in s.pieces[g]:
                                reduce(*two, *piece)
                        if g in s.on_dve:
                            sub(i, r, g)
                        if g == s.fetch_at and ahead >= 1:
                            fetch_max(*one)
                        if g == s.divide_at and (type(i) is not int or i or r):
                            divide(*before)

                dve.sem_inc(s.nrm_done, 2)
                dve.sem_inc(s.red_done, 2)
                dve.sem_inc(s.mf_ready, 2)
                for piece in s.all_pieces:
                    reduce(0, 0, *piece)
                fetch_max(0, 0)
                for piece in s.all_pieces:
                    reduce(0, 1, *piece)
                rounds(lambda count: st.loop(count, 2 * RING), step)
                divide(HEADS // RING - 1, RING - 1)
                for j in range(NB):
                    dve.wait_ge(s.wo_done, j + 1)
                    t = slice(j * TPB, (j + 1) * TPB)
                    src = ps[:, 2 + j % 2, :].rearrange("p (t d) -> p t d", d=D)
                    if rope:
                        link(v.tensor_tensor(x[:, t, :], x[:, t, :], bcast(bo[:], 1, TPB), ALU.add))
                    v.tensor_tensor(x[:, t, :], src, x[:, t, :], ALU.add).then_inc(s.wo_free, 1)
                dve.wait_ge(s.wo_free, NB)

            for s in S:
                (ffn if s.kind.startswith("ffn") else attention)(s)
                dve.sem_inc(stage_done, 1)


N_SMALL = 16
STAGES = ("ffn0", "attn0", "ffn0", "ffn1", "attn1", "ffn1")


def constants():
    p, c = np.arange(P)[:, None], np.arange(P)[None, :]
    consts = np.zeros((P, CONST_COLS), np.float32)
    consts[:, 0:P] = p == c
    consts[:, P:2 * P] = p < c
    consts[:, 2 * P:3 * P] = np.where(c > p, NEG, 0)
    consts[:, 3 * P:4 * P] = np.where(p > c, NEG, 0)
    consts[:, 4 * P:4 * P + E] = E - np.arange(E)[None, :]
    consts[:, 4 * P + E:4 * P + 2 * E] = CAPACITY * np.arange(E)[None, :]
    consts[:, 4 * P + 2 * E:4 * P + 2 * E + TILES[0]] = TS * np.arange(TILES[0])[None, :]
    o = 4 * P + 2 * E + TILES[0]
    consts[:, o:o + P] = c
    consts[:, o + P:o + P + HALVES] = P * np.arange(HALVES)[None, :]
    consts[:, o + P + HALVES:o + P + 2 * HALVES] = 2 * T + P * np.arange(HALVES)[None, :] + p
    consts[:, o + P + 2 * HALVES:] = 1 + np.arange(2 * NT)[None, :]
    inv = (1.0 / np.float32(10000.0) ** (np.arange(0, DH, 2, dtype=np.float32) / np.float32(DH))).astype(np.float32)
    ang = np.repeat(np.arange(N, dtype=np.float32)[:, None] * inv[None, :], 2, axis=-1)
    sign = np.where(np.arange(DH) % 2 == 0, -1.0, 1.0).astype(np.float32)
    cos, sin = np.cos(ang).astype(np.float32), (np.sin(ang) * sign).astype(np.float32)
    trig = np.stack([np.tile(cos.T, (H, 1)), np.tile(sin.T, (H, 1))], axis=1)
    return consts, np.ascontiguousarray(trig)


def kernel(**inputs):
    import concourse.bacc as bacc
    from concourse.bass_utils import run_bass_kernel_spmd as run

    a = {k: np.asarray(v) for k, v in inputs.items()}
    swap = np.arange(D) ^ 1
    consts, trig = constants()
    wq, wk, wv = (a[f"L0_attn_W{k}"] for k in "qkv")
    bq, bk = a["L0_attn_bq"], a["L0_attn_bk"]
    arrays = {
        "x": a["L0_attn_x"].reshape(T, D),
        "consts": consts,
        "trig": trig,
        "rb": a["L0_ffn_router_b"],
        "rw0": a["L0_ffn_router_w"].T,
        "rw1": a["L1_ffn_w_router"],
        "lnw": a["L0_ffn_ln_w"],
        "lnb": a["L0_ffn_ln_b"],
        "ffn_bias": a["L1_ffn_bias"].reshape(D),
        "experts0": np.concatenate([
            a["L0_ffn_w1"].transpose(0, 2, 1),
            a["L0_ffn_w2"].reshape(E, D, NC, P).transpose(0, 3, 2, 1).reshape(E, P, NC * D),
            a["L0_ffn_b1"].reshape(E, NC, P).transpose(0, 2, 1),
            np.broadcast_to(a["L0_ffn_b2"][:, None, :], (E, P, D))], axis=2),
        "experts1": np.concatenate([
            a["L1_ffn_w1"],
            a["L1_ffn_w2"].reshape(E, NC, P, D).transpose(0, 2, 1, 3).reshape(E, P, NC * D)], axis=2),
        "wqkv": np.stack([wq, wq[:, swap], wk, wk[:, swap], wv], axis=1),
        "bqk": np.stack([bq, bq[swap], bk, bk[swap]], axis=1),
        "bv": a["L0_attn_bv"],
        "bo": a["L0_attn_bo"],
        "wo0": a["L0_attn_Wo"],
        "wo1": a["L1_attn_W_o"],
        "wd": np.stack([a["L1_attn_W_dq"], a["L1_attn_W_dkv"]], axis=1),
        "wu": np.stack([a["L1_attn_W_uq"], a["L1_attn_W_uk"], a["L1_attn_W_uv"]], axis=1),
    }
    nc = bacc.Bacc("TRN2", target_bir_lowering=False, num_devices=1)
    maps, ins = {}, {}
    for name, v in arrays.items():
        v = np.ascontiguousarray(v)
        maps[f"in_{name}"] = v
        ins[name] = nc.dram_tensor(f"in_{name}", v.shape, mybir.dt.from_np(v.dtype), kind="ExternalInput").ap()
    out = nc.dram_tensor("out", (T, D), F32, kind="ExternalOutput").ap()
    build(nc, ins, out, STAGES)
    r = run(nc, [maps], core_ids=[0])
    return r.results[0]["out"].reshape(B, N, D)
```
